# Optimizing a Trainium2 kernel written in Bass

```python
import numpy as np
import jax
import jax.numpy as jnp

def _softmax(x, axis=-1):
    return jax.nn.softmax(x, axis=axis)

def _gelu(x):
    return jax.nn.gelu(x, approximate=True)

def _silu(x):
    return jax.nn.silu(x)

def _sigmoid(x):
    return jax.nn.sigmoid(x)

def _layernorm(x, axis=-1, eps=1e-05):
    m = jnp.mean(x, axis=axis, keepdims=True)
    v = jnp.var(x, axis=axis, keepdims=True)
    return (x - m) / jnp.sqrt(v + eps)

def _scatter_add(tgt, idx, src, axis=0):
    return tgt.at[idx].add(src)

def _segment_sum(src, seg, n):
    return jax.ops.segment_sum(src, seg, n)
kernel_name = 'mk_xattn_ffn_d2_seqx_r4_dc424d'

def setup_inputs(seed: int=0):
    np.random.seed(seed)
    _w = jnp.asarray

    def _rec_inputs():
        import jax
        import jax.numpy as jnp
        _rk = jax.random.key(seed)
        x = 0.002226 + 0.9996 * jax.random.normal(jax.random.fold_in(_rk, 1), (16, 256, 256), jnp.float32)
        _lenS = 256 - jax.random.randint(jax.random.fold_in(_rk, 7), (16,), 0, max(1, 256 // 4) + 1, jnp.int32)
        _lenS2 = 256 - jax.random.randint(jax.random.fold_in(_rk, 8), (16,), 0, max(1, 256 // 4) + 1, jnp.int32)
        _ctx_1024P = jax.random.normal(jax.random.fold_in(_rk, 11), (16, 16, 256), jnp.float32)
        _ctx_1024c = jax.random.dirichlet(jax.random.fold_in(_rk, 511), 0.3 * jnp.ones((16,), jnp.float32), (16, 256))
        _ctx_1024t = jnp.einsum('bsk,bkd->bsd', _ctx_1024c, _ctx_1024P)
        _ctx_1024t = _ctx_1024t * jax.lax.rsqrt(jnp.mean(jnp.square(_ctx_1024t)) + 1e-12) * 0.953939
        ctx_1024 = -0.000125008 + 0.999885 * (_ctx_1024t + 0.3 * jax.random.normal(jax.random.fold_in(_rk, 611), (16, 256, 256), jnp.float32))
        return (x, ctx_1024)
    x, ctx_1024 = _rec_inputs()

    def _L0_xattn_setup():
        import jax, jax.numpy as jnp
        import numpy as np
        B, M, N, DIM, DH, H = (8, 1024, 64, 256, 128, 8)
        INNER = DH * H
        EPS = 1e-05

        def _layernorm(x, g, b):
            mu = jnp.mean(x, axis=-1, keepdims=True)
            var = jnp.var(x, axis=-1, keepdims=True)
            return (x - mu) * jax.lax.rsqrt(var + EPS) * g + b
        key = jax.random.key(seed)
        ks = jax.random.split(key, 8)
        sd = 0.02
        return {'x': jax.random.normal(ks[0], (B, M, DIM), jnp.float32), 'latents': jax.random.normal(ks[1], (B, N, DIM), jnp.float32), 'gamma_media': jnp.ones((DIM,), jnp.float32), 'beta_media': jnp.zeros((DIM,), jnp.float32), 'gamma_lat': jnp.ones((DIM,), jnp.float32), 'beta_lat': jnp.zeros((DIM,), jnp.float32), 'Wq': jax.random.normal(ks[2], (DIM, INNER), jnp.float32) * sd, 'bq': jnp.zeros((INNER,), jnp.float32), 'Wkv': jax.random.normal(ks[3], (DIM, 2 * INNER), jnp.float32) * sd, 'bkv': jnp.zeros((2 * INNER,), jnp.float32), 'Wo': jax.random.normal(ks[4], (INNER, DIM), jnp.float32) * sd, 'bo': jnp.zeros((DIM,), jnp.float32)}
    _L0_xattn_all = _L0_xattn_setup()
    _L0_xattn_in = {k: v for k, v in _L0_xattn_all.items() if k in ('gamma_media', 'beta_media', 'gamma_lat', 'beta_lat', 'Wq', 'bq', 'Wkv', 'bkv', 'Wo', 'bo')}
    del _L0_xattn_all

    def _L0_ffn_setup():
        import jax, jax.numpy as jnp
        import numpy as np
        LORA_DIM = 16
        LORA_TOKEN_INDEX = 1
        B, S, D, H = (4, 512, 256, 1024)
        key = jax.random.key(seed)
        ks = jax.random.split(key, 6)
        x = jax.random.normal(ks[0], (B, S, D), dtype=jnp.float32)
        W1 = jax.random.normal(ks[1], (H, D), dtype=jnp.float32) * 0.02
        b1 = jnp.zeros((H,), dtype=jnp.float32)
        W2 = jax.random.normal(ks[2], (D, H), dtype=jnp.float32) * 0.02
        b2 = jnp.zeros((D,), dtype=jnp.float32)
        scale = jnp.asarray(0.001, dtype=jnp.float32)
        return {'x': x, 'W1': W1, 'b1': b1, 'W2': W2, 'b2': b2, 'scale': scale}
    _L0_ffn_all = _L0_ffn_setup()
    _L0_ffn_in = {k: v for k, v in _L0_ffn_all.items() if k in ('W1', 'b1', 'W2', 'b2', 'scale')}
    del _L0_ffn_all

    def _L1_xattn_setup():
        import jax, jax.numpy as jnp
        import numpy as np
        B, S, DIN, DK, DV = (8, 512, 256, 256, 256)
        key = jax.random.key(seed)
        ks = jax.random.split(key, 9)
        s_in = 1.0 / np.sqrt(DIN)
        return {'query': jax.random.normal(ks[0], (B, S, DIN), jnp.float32), 'key_': jax.random.normal(ks[1], (B, S, DIN), jnp.float32), 'value': jax.random.normal(ks[2], (B, S, DIN), jnp.float32), 'Wq_w': jax.random.uniform(ks[3], (DK, DIN), jnp.float32, -s_in, s_in), 'Wq_b': jax.random.uniform(ks[4], (DK,), jnp.float32, -s_in, s_in), 'Wk_w': jax.random.uniform(ks[5], (DK, DIN), jnp.float32, -s_in, s_in), 'Wk_b': jax.random.uniform(ks[6], (DK,), jnp.float32, -s_in, s_in), 'Wv_w': jax.random.uniform(ks[7], (DV, DIN), jnp.float32, -s_in, s_in), 'Wv_b': jax.random.uniform(ks[8], (DV,), jnp.float32, -s_in, s_in)}
    _L1_xattn_all = _L1_xattn_setup()
    _L1_xattn_in = {k: v for k, v in _L1_xattn_all.items() if k in ('Wq_w', 'Wq_b', 'Wk_w', 'Wk_b', 'Wv_w', 'Wv_b')}
    del _L1_xattn_all

    def _L1_ffn_setup():
        import jax, jax.numpy as jnp
        import numpy as np
        import math
        GOLDEN_CENTER = 1.0 / math.e
        GOLDEN_LOWER = 0.5 - math.log(4.0 / 3.0)
        GOLDEN_UPPER = 0.5
        B, T, D = (4, 512, 256)
        E = 8
        I = 1024 // (E // 2)

        def _routing_weights(x, Wr, temperature):
            inh = jax.nn.sigmoid(x @ Wr / temperature)
            in_zone = (inh >= GOLDEN_LOWER) & (inh <= GOLDEN_UPPER)
            dist = jnp.abs(inh - GOLDEN_CENTER)
            w = jnp.exp(-dist / 0.1) * in_zone.astype(x.dtype)
            wsum = w.sum(axis=-1, keepdims=True)
            no_expert = wsum < 1e-08
            fb = jnp.exp(-dist / 0.3)
            _, top2 = jax.lax.top_k(fb, 2)
            fb_mask = jax.nn.one_hot(top2, E, dtype=x.dtype).sum(axis=-2)
            fb_w = fb * fb_mask
            fb_w = fb_w / jnp.clip(fb_w.sum(axis=-1, keepdims=True), 1e-08)
            w = jnp.where(no_expert, fb_w, w)
            wsum = w.sum(axis=-1, keepdims=True)
            return w / jnp.clip(wsum, 1e-08)
        key = jax.random.key(seed)
        k = jax.random.split(key, 6)
        s_d = 1.0 / math.sqrt(D)
        s_i = 1.0 / math.sqrt(I)
        return {'x': jax.random.normal(k[0], (B, T, D), jnp.float32), 'Wg': jax.random.normal(k[1], (E, D, I), jnp.float32) * s_d, 'Wu': jax.random.normal(k[2], (E, D, I), jnp.float32) * s_d, 'Wd': jax.random.normal(k[3], (E, I, D), jnp.float32) * s_i, 'Wr': jax.random.normal(k[4], (D, E), jnp.float32) * s_d, 'temperature': jnp.ones((1,), jnp.float32)}
    _L1_ffn_all = _L1_ffn_setup()
    _L1_ffn_in = {k: v for k, v in _L1_ffn_all.items() if k in ('Wg', 'Wu', 'Wd', 'Wr', 'temperature')}
    del _L1_ffn_all
    return {'x': x, 'ctx_1024': ctx_1024, 'L0_xattn_gamma_media': _L0_xattn_in['gamma_media'], 'L0_xattn_beta_media': _L0_xattn_in['beta_media'], 'L0_xattn_gamma_lat': _L0_xattn_in['gamma_lat'], 'L0_xattn_beta_lat': _L0_xattn_in['beta_lat'], 'L0_xattn_Wq': _L0_xattn_in['Wq'], 'L0_xattn_bq': _L0_xattn_in['bq'], 'L0_xattn_Wkv': _L0_xattn_in['Wkv'], 'L0_xattn_bkv': _L0_xattn_in['bkv'], 'L0_xattn_Wo': _L0_xattn_in['Wo'], 'L0_xattn_bo': _L0_xattn_in['bo'], 'L0_ffn_W1': _L0_ffn_in['W1'], 'L0_ffn_b1': _L0_ffn_in['b1'], 'L0_ffn_W2': _L0_ffn_in['W2'], 'L0_ffn_b2': _L0_ffn_in['b2'], 'L0_ffn_scale': _L0_ffn_in['scale'], 'L1_xattn_Wq_w': _L1_xattn_in['Wq_w'], 'L1_xattn_Wq_b': _L1_xattn_in['Wq_b'], 'L1_xattn_Wk_w': _L1_xattn_in['Wk_w'], 'L1_xattn_Wk_b': _L1_xattn_in['Wk_b'], 'L1_xattn_Wv_w': _L1_xattn_in['Wv_w'], 'L1_xattn_Wv_b': _L1_xattn_in['Wv_b'], 'L1_ffn_Wg': _L1_ffn_in['Wg'], 'L1_ffn_Wu': _L1_ffn_in['Wu'], 'L1_ffn_Wd': _L1_ffn_in['Wd'], 'L1_ffn_Wr': _L1_ffn_in['Wr'], 'L1_ffn_temperature': _L1_ffn_in['temperature']}

def reference(x, ctx_1024, L0_xattn_gamma_media, L0_xattn_beta_media, L0_xattn_gamma_lat, L0_xattn_beta_lat, L0_xattn_Wq, L0_xattn_bq, L0_xattn_Wkv, L0_xattn_bkv, L0_xattn_Wo, L0_xattn_bo, L0_ffn_W1, L0_ffn_b1, L0_ffn_W2, L0_ffn_b2, L0_ffn_scale, L1_xattn_Wq_w, L1_xattn_Wq_b, L1_xattn_Wk_w, L1_xattn_Wk_b, L1_xattn_Wv_w, L1_xattn_Wv_b, L1_ffn_Wg, L1_ffn_Wu, L1_ffn_Wd, L1_ffn_Wr, L1_ffn_temperature):
    import jax
    import jax.numpy as jnp

    def _L0_xattn_ref(x, latents, gamma_media, beta_media, gamma_lat, beta_lat, Wq, bq, Wkv, bkv, Wo, bo):
        import jax, jax.numpy as jnp
        import numpy as np
        B, M, N, DIM, DH, H = (8, 1024, 64, 256, 128, 8)
        INNER = DH * H
        EPS = 1e-05

        def _layernorm(x, g, b):
            mu = jnp.mean(x, axis=-1, keepdims=True)
            var = jnp.var(x, axis=-1, keepdims=True)
            return (x - mu) * jax.lax.rsqrt(var + EPS) * g + b
        b = x.shape[0]
        xn = _layernorm(x, gamma_media, beta_media)
        ln = _layernorm(latents, gamma_lat, beta_lat)
        q = ln @ Wq + bq
        kv_input = jnp.concatenate([xn, ln], axis=1)
        kv = kv_input @ Wkv + bkv
        k, v = jnp.split(kv, 2, axis=-1)

        def to_heads(t):
            return t.reshape(b, t.shape[1], H, DH).transpose(0, 2, 1, 3)
        q, k, v = (to_heads(q), to_heads(k), to_heads(v))
        q = q * DH ** (-0.5)
        sim = jnp.einsum('bhid,bhjd->bhij', q, k)
        attn = jax.nn.softmax(sim, axis=-1)
        out = jnp.einsum('bhij,bhjd->bhid', attn, v)
        out = out.transpose(0, 2, 1, 3).reshape(b, -1, INNER)
        return out @ Wo + bo

    def _L0_ffn_ref(x, W1, b1, W2, b2, scale):
        import jax, jax.numpy as jnp
        import numpy as np
        LORA_DIM = 16
        LORA_TOKEN_INDEX = 1
        B, S, D, H = (4, 512, 256, 1024)
        Bx, Sx, Dx = x.shape
        Hx = W1.shape[0]
        lt = jax.lax.dynamic_slice_in_dim(x, LORA_TOKEN_INDEX, LORA_DIM, axis=1)
        even = lt[:, ::2, :]
        odd = lt[:, 1::2, :]
        m1 = (even[:, :4, :, None] * odd[:, :4, None, :]).reshape(Bx, Hx, Dx)
        m2 = (even[:, 4:, :, None] * odd[:, 4:, None, :]).reshape(Bx, Dx, Hx)
        h = jnp.einsum('bsd,hd->bsh', x, W1) + scale * jnp.einsum('bsd,bhd->bsh', x, m1) + b1
        h = jax.nn.gelu(h, approximate=False)
        out = jnp.einsum('bsh,oh->bso', h, W2) + scale * jnp.einsum('bsh,boh->bso', h, m2) + b2
        return out

    def _L1_xattn_ref(query, key_, value, Wq_w, Wq_b, Wk_w, Wk_b, Wv_w, Wv_b):
        import jax, jax.numpy as jnp
        import numpy as np
        B, S, DIN, DK, DV = (8, 512, 256, 256, 256)
        Q = jnp.einsum('bsd,kd->bsk', query, Wq_w) + Wq_b
        K = jnp.einsum('bsd,kd->bsk', key_, Wk_w) + Wk_b
        V = jnp.einsum('bsd,vd->bsv', value, Wv_w) + Wv_b
        scale = 1.0 / jnp.sqrt(jnp.asarray(Q.shape[-1], Q.dtype))
        scores = jnp.einsum('bqk,bsk->bqs', Q, K) * scale
        attn = jax.nn.softmax(scores, axis=-1)
        return jnp.einsum('bqs,bsv->bqv', attn, V)

    def _L1_ffn_ref(x, Wg, Wu, Wd, Wr, temperature):
        import jax, jax.numpy as jnp
        import numpy as np
        import math
        GOLDEN_CENTER = 1.0 / math.e
        GOLDEN_LOWER = 0.5 - math.log(4.0 / 3.0)
        GOLDEN_UPPER = 0.5
        B, T, D = (4, 512, 256)
        E = 8
        I = 1024 // (E // 2)

        def _routing_weights(x, Wr, temperature):
            inh = jax.nn.sigmoid(x @ Wr / temperature)
            in_zone = (inh >= GOLDEN_LOWER) & (inh <= GOLDEN_UPPER)
            dist = jnp.abs(inh - GOLDEN_CENTER)
            w = jnp.exp(-dist / 0.1) * in_zone.astype(x.dtype)
            wsum = w.sum(axis=-1, keepdims=True)
            no_expert = wsum < 1e-08
            fb = jnp.exp(-dist / 0.3)
            _, top2 = jax.lax.top_k(fb, 2)
            fb_mask = jax.nn.one_hot(top2, E, dtype=x.dtype).sum(axis=-2)
            fb_w = fb * fb_mask
            fb_w = fb_w / jnp.clip(fb_w.sum(axis=-1, keepdims=True), 1e-08)
            w = jnp.where(no_expert, fb_w, w)
            wsum = w.sum(axis=-1, keepdims=True)
            return w / jnp.clip(wsum, 1e-08)
        weights = _routing_weights(x, Wr, temperature)
        gate = jnp.einsum('btd,edi->beti', x, Wg)
        up = jnp.einsum('btd,edi->beti', x, Wu)
        h = jax.nn.silu(gate) * up
        e_out = jnp.einsum('beti,eid->betd', h, Wd)
        out = jnp.einsum('bte,betd->btd', weights, e_out)
        return out
    x = x + _L0_xattn_ref(ctx_1024, _layernorm(x, axis=-1), L0_xattn_gamma_media, L0_xattn_beta_media, L0_xattn_gamma_lat, L0_xattn_beta_lat, L0_xattn_Wq, L0_xattn_bq, L0_xattn_Wkv, L0_xattn_bkv, L0_xattn_Wo, L0_xattn_bo)
    x = x + _L0_ffn_ref(_layernorm(x, axis=-1), L0_ffn_W1, L0_ffn_b1, L0_ffn_W2, L0_ffn_b2, L0_ffn_scale)
    x = x + _L1_xattn_ref(_layernorm(x, axis=-1), ctx_1024, ctx_1024, L1_xattn_Wq_w, L1_xattn_Wq_b, L1_xattn_Wk_w, L1_xattn_Wk_b, L1_xattn_Wv_w, L1_xattn_Wv_b)
    x = x + _L1_ffn_ref(_layernorm(x, axis=-1), L1_ffn_Wg, L1_ffn_Wu, L1_ffn_Wd, L1_ffn_Wr, L1_ffn_temperature)
    return x

_drawn_inputs = setup_inputs


def setup_inputs(seed=0):
    import zlib

    import numpy as np

    out = dict(_drawn_inputs(seed))
    spreads = {'L0_xattn_gamma_media': (1.0, 0.2),
     'L0_xattn_beta_media': (0.0, 0.441),
     'L0_xattn_gamma_lat': (1.0, 0.6),
     'L0_xattn_beta_lat': (0.0, 0.276),
     'L0_xattn_bq': (0.0, 0.8),
     'L0_xattn_bkv': (0.0, 0.1),
     'L0_xattn_bo': (0.0, 0.1),
     'L0_ffn_b1': (0.0, 0.1),
     'L0_ffn_b2': (0.0, 0.1)}
    factors = {'L0_xattn_Wq': 3.463, 'L1_xattn_Wq_b': 5.348, 'L1_xattn_Wk_b': 64.0}
    for name, (base, spread) in spreads.items():
        noise = np.random.default_rng([zlib.crc32(name.encode()), seed]).standard_normal(out[name].shape)
        drawn = base * np.exp(spread * noise) if base else spread * noise
        out[name] = jnp.asarray(drawn.astype(out[name].dtype))
    for name, factor in factors.items():
        out[name] = (out[name] * factor).astype(out[name].dtype)
    return out
```

```python
import concourse.bass as bass
from concourse import mybir
from contextlib import ExitStack

F32 = mybir.dt.float32
F32R = mybir.dt.float32r
ACT = mybir.ActivationFunctionType
ALU = mybir.AluOpType
AX = mybir.AxisListType

P = 128
B = 16
S = 256
D = 256
ST = S // P
DC = D // P
EPS = 1e-5


def f32(ap):
    return ap.bitcast(F32)


class Order:

    def __init__(self, names, first, before=None, step=0, turn=None):
        self.names, self.first, self.before = names, first, before
        self.step, self.turn = step, turn

    def at(self, i):
        return self.first + i if self.turn is None else self.first + i + self.turn * self.step

    def bank(self, i, banks):
        return (self.first + i) % banks

    def done(self, name, i):
        if name in self.names[:i]:
            return self.at(len(self.names[:i]) - 1 - self.names[:i][::-1].index(name)) + 1
        back = self.before.index_from_end(name)
        return self.at(-back) + 1

    def index_from_end(self, name):
        return self.names[::-1].index(name) + 1


def latent_attention(nc, x, ctx_in, x1, g_media, b_media, g_lat, b_lat, Wq, bq, Wkv, bkv, Wo, bo):
    H = 8
    DH = Wq.shape[1] // H
    INNER = H * DH
    KT = 2 * ST
    SK = KT * P
    QSCALE = float(DH) ** -0.5
    RING = 4
    HALF = INNER // 2

    def slot(h, prev, nxt):
        out = []
        if h + 2 < H or nxt:
            out.append(("K", (h + 2) % H))
        if h > 0 or prev:
            out.append(("O", (h - 1) % H))
        if h % 2 == 0 and (h + 2 < H or nxt):
            out.append(("Q", (h // 2 + 1) % (H // 2)))
        if h < KT:
            out.append(("V", KT + h))
        if h >= H - 2 and nxt:
            out += [("V", 2 * (h - H + 2)), ("V", 2 * (h - H + 2) + 1)]
        return out + [("T", h, 0), ("T", h, 1)]

    def turn_fills(prev, nxt):
        return [f for h in range(H) for f in slot(h, prev, nxt)]

    start = [("K", 0), ("Q", 0), ("K", 1)] + [("V", j) for j in range(KT)]
    sections = {}
    sections["start"] = Order(start, 0)
    sections["first"] = Order(turn_fills(False, True), len(start), sections["start"])
    loop_first = len(start) + len(sections["first"].names)
    loop_names = turn_fills(True, True)
    F = len(loop_names)
    assert F % RING == 0
    TURNS = B - 2
    tail_first = loop_first + F * TURNS

    ctx = ExitStack()
    with ctx:
        def sb(name, shape, dt=F32):
            return ctx.enter_context(nc.sbuf_tensor("a_" + name, shape, dt))

        def pb(name, shape):
            return ctx.enter_context(nc.psum_tensor("a_" + name, shape, F32))

        def sem(name):
            return ctx.enter_context(nc.semaphore("a_" + name))

        wqh, wql = sb("wqh", [P, DC, INNER], F32R), sb("wql", [P, DC, INNER], F32R)
        wkvh, wkvl = sb("wkvh", [P, DC, 2 * INNER], F32R), sb("wkvl", [P, DC, 2 * INNER], F32R)
        woh, wol = sb("woh", [P, H, D], F32R), sb("wol", [P, H, D], F32R)
        stage_q = sb("stage_q", [P, DC, INNER])
        stage_kv = sb("stage_kv", [P, DC, 2 * INNER])
        stage_o = sb("stage_o", [P, H, D])
        gm, bm = sb("gm", [P, DC]), sb("bm", [P, DC])
        gl, bl = sb("gl", [P, DC]), sb("bl", [P, DC])
        bq_raw, bq_s = sb("bq_raw", [P, H]), sb("bq_s", [P, H])
        bkv_s = sb("bkv_s", [P, 2, H])
        bo_b = sb("bo_b", [P, D])
        ident = sb("ident", [P, P])
        mhalf = sb("mhalf", [P, ST])
        x_in, c_in = sb("x_in", [P, ST, D]), sb("c_in", [P, ST, D])
        x_ln, x_ln2, c_ln = sb("x_ln", [P, ST, D]), sb("x_ln2", [P, ST, D]), sb("c_ln", [P, ST, D])
        x_res, x_out = sb("x_res", [P, ST, D]), sb("x_out", [P, ST, D])
        stats = sb("stats", [P, 3, ST, 6])
        mv = sb("mv", [P, 3, ST, 2])
        veps, rstd = sb("veps", [P, 3, ST]), sb("rstd", [P, 3, ST])
        aff = sb("aff", [P, 2, DC, S])
        kvh, kvl = sb("kvh", [P, DC, SK], F32R), sb("kvl", [P, DC, SK], F32R)
        kth, ktl = sb("kth", [P, 2, SK], F32R), sb("ktl", [P, 2, SK], F32R)
        qth, qtl = sb("qth", [P, 2, 2, S], F32R), sb("qtl", [P, 2, 2, S], F32R)
        vh, vl = sb("vh", [P, KT, INNER], F32R), sb("vl", [P, KT, INNER], F32R)
        pr = sb("pr", [P, 2, ST, SK])
        pth, ptl = sb("pth", [P, KT, S], F32R), sb("ptl", [P, KT, S], F32R)
        oth, otl = sb("oth", [P, H, S], F32R), sb("otl", [P, H, S], F32R)
        nmax, rsum, rinv = sb("nmax", [P, 2, ST]), sb("rsum", [P, 2, ST]), sb("rinv", [P, 2, ST])

        ring = [pb(f"ring{i}", [P, 512]) for i in range(RING)]
        sim = [pb(f"sim{i}", [P, SK]) for i in range(ST)]
        ps_c = pb("ps_c", [P, DC, S])
        ps_x = pb("ps_x", [P, 512])

        w_in = [sem(f"w_in{i}") for i in range(3)]
        c_small = sem("c_small")
        consts = sem("consts")
        w_hi, w_lo = sem("w_hi"), sem("w_lo")
        ring_full, ring_hi, ring_lo = sem("ring_full"), sem("ring_hi"), sem("ring_lo")
        in_x, in_c, in_res = sem("in_x"), sem("in_c"), sem("in_res")
        dve_step, pool_step, took = sem("dve_step"), sem("pool_step"), sem("took")
        var_ready, rstd_ready = sem("var_ready"), sem("rstd_ready")
        ln_ready, lnT_ready, aff_ready, kv_ready = sem("ln_ready"), sem("lnT_ready"), sem("aff_ready"), sem("kv_ready")
        kv_hi = sem("kv_hi")
        sim_full, max_ready, exp_done, inv_ready, prob_ready, prob_used = (
            sem(n) for n in ("sim_full", "max_ready", "exp_done", "inv_ready", "prob_ready", "prob_used"))
        wo_full, res_ready, x1_ready, x1_out = sem("wo_full"), sem("res_ready"), sem("x1_ready"), sem("x1_out")

        def sections_of(eng, body):
            body(sections["first"], 0, False, True)
            with eng.Fori(1, B - 1) as b:
                body(Order(loop_names, loop_first - F, sections["first"], F, b), b, True, True)
            loop = Order(loop_names, 0)
            body(Order(turn_fills(True, False), tail_first, loop), B - 1, True, False)

        x_t = x.rearrange("b (t p) d -> b p t d", p=P)
        c_t = ctx_in.rearrange("b (t p) d -> b p t d", p=P)
        x1_t = x1.rearrange("b (t p) d -> b p t d", p=P)

        block = ctx.enter_context(nc.Block())

        @block.sync
        def _(sp):
            sp.dma_start(c_in[:], c_t[0]).then_inc(in_c, 16)
            sp.dma_start(x_in[:], x_t[0]).then_inc(in_x, 16)
            for k, (w, n) in enumerate(((g_media, gm), (b_media, bm), (g_lat, gl), (b_lat, bl))):
                sp.dma_start(n[:], w).then_inc(c_small, 16)
            sp.dma_start(bq_raw[:], bq).then_inc(c_small, 16)
            sp.dma_start(bkv_s[:], bkv).then_inc(c_small, 16)
            sp.dma_start(bo_b[:], bo.to_broadcast([P, D])).then_inc(c_small, 16)
            sp.dma_start(stage_kv[:], Wkv.rearrange("(c p) n -> p c n", p=P)).then_inc(w_in[0], 16)
            sp.dma_start(stage_q[:], Wq.rearrange("(c p) n -> p c n", p=P)).then_inc(w_in[1], 16)
            sp.dma_start(stage_o[:], Wo.rearrange("(h p) n -> p h n", p=P)).then_inc(w_in[2], 16)

            def turn(order, b, prev, nxt):
                if nxt:
                    sp.wait_ge(ln_ready, b * 3 + 3)
                    sp.dma_start(c_in[:], c_t[b + 1]).then_inc(in_c, 16)
                    sp.dma_start(x_in[:], x_t[b + 1]).then_inc(in_x, 16)
                if prev:
                    sp.wait_ge(x1_ready, b)
                    sp.dma_start(x1_t[b - 1], x_out[:]).then_inc(x1_out, 16)
                sp.dma_start(x_res[:], x_t[b]).then_inc(in_res, 16)
            sections_of(sp, turn)
            sp.wait_ge(x1_ready, B)
            sp.dma_start(x1_t[B - 1], x_out[:]).then_inc(x1_out, 16)
            sp.wait_ge(x1_out, 16 * B)

        @block.gpsimd
        def _(pool):
            def take(s, value):
                pool.wait_ge(s, value)
                pool.sem_inc(took, 1)

            nc.gpsimd.memset(ident[:], 0.0).then_inc(pool_step, 1)
            nc.gpsimd.memset(mhalf[:], -0.5).then_inc(pool_step, 1)
            pool.wait_ge(pool_step, 2)
            nc.gpsimd.affine_select(out=ident[:], in_=ident[:], compare_op=ALU.not_equal, fill=1.0, base=0,
                                    pattern=[[-1, P]], channel_multiplier=1).then_inc(consts, 1)
            pool.wait_ge(c_small, 16 * 7)

            def rstd_of(b, k):
                take(var_ready, b * 3 + k + 1)
                nc.gpsimd.tensor_scalar(veps[:, k, :], mv[:, k, :, 1], EPS, 1.0, ALU.add, ALU.mult)\
                    .then_inc(pool_step, 1)
                pool.wait_ge(pool_step, b * 3 + k + 3)
                nc.gpsimd.tensor_tensor(rstd[:, k, :], veps[:, k, :], mhalf[:], ALU.pow).then_inc(rstd_ready, 1)

            def normalise_probs(b, h):
                for t in range(ST):
                    take(inv_ready, (b * H + h) * ST + t + 1)
                    nc.gpsimd.tensor_scalar(pr[:, h % 2, t, :], pr[:, h % 2, t, :], rinv[:, h % 2, t:t + 1], 1.0,
                                            ALU.mult, ALU.mult).then_inc(prob_ready, 1)

            for k in range(3):
                rstd_of(0, k)
            normalise_probs(0, 0)

            def turn(order, b, prev, nxt):
                for h in range(H):
                    if h == 1:
                        pool.wait_ge(in_res, b * 16 + 16)
                        if prev:
                            pool.wait_ge(x1_ready, b)
                        nc.gpsimd.tensor_tensor(x_res[:], x_res[:], bo_b[:].unsqueeze(1).to_broadcast([P, ST, D]),
                                                ALU.add).then_inc(res_ready, 1)
                    if nxt and h in (2, 3, 4):
                        rstd_of(b + 1, h - 2)
                    if h + 1 < H:
                        normalise_probs(b, h + 1)
                    elif nxt:
                        normalise_probs(b + 1, 0)
            sections_of(pool, turn)

        @block.scalar
        def _(act):
            act.wait_ge(w_in[0], 16)
            for c in range(DC):
                nc.scalar.activation(wkvh[:, c], stage_kv[:, c], ACT.Copy).then_inc(w_hi, 1)
            act.wait_ge(c_small, 16 * 7)

            def affine(b):
                for k, (ps, g, bb) in enumerate(((ps_c, gm, bm), (ps_x, gl, bl))):
                    act.wait_ge(lnT_ready, b * 2 + k + 1)
                    for c in range(DC):
                        src = ps_c[:, c, :] if k == 0 else ps_x[:, c * S:(c + 1) * S]
                        nc.scalar.activation(aff[:, k, c, :], src, ACT.Identity, bias=bb[:, c:c + 1],
                                             scale=g[:, c:c + 1]).then_inc(aff_ready, 1)

            affine(0)
            act.wait_ge(w_in[1], 16)
            nc.scalar.activation(bq_s[:], bq_raw[:], ACT.Copy, scale=QSCALE).then_inc(w_hi, 1)
            nc.scalar.activation(wqh[:], stage_q[:], ACT.Copy, scale=QSCALE).then_inc(w_hi, 1)
            act.wait_ge(w_in[2], 16)
            nc.scalar.activation(woh[:], stage_o[:], ACT.Copy).then_inc(w_hi, 1)
            act.wait_ge(w_hi, DC + 3)

            def high_half(order, i):
                name = order.names[i]
                bank = ring[order.bank(i, RING)]
                act.wait_ge(ring_full, order.at(i) + 1)
                h = name[1]
                if name[0] == "K":
                    nc.scalar.activation(kth[:, h % 2], bank[:], ACT.Identity, bias=bkv_s[:, 0, h:h + 1])\
                        .then_inc(ring_hi, 1)
                elif name[0] == "Q":
                    for j in range(2):
                        last = nc.scalar.activation(qth[:, h % 2, j], bank[:, j * S:(j + 1) * S], ACT.Identity,
                                                    bias=bq_s[:, 2 * h + j:2 * h + j + 1])
                    last.then_inc(ring_hi, 1)
                elif name[0] == "V":
                    nc.scalar.activation(vh[:, h % KT, h // KT * HALF:(h // KT + 1) * HALF], bank[:], ACT.Copy)\
                        .then_inc(ring_hi, 1)
                elif name[0] == "T":
                    nc.scalar.activation(pth[:, :, name[2] * P:(name[2] + 1) * P],
                                         bank[:].rearrange("p (k q) -> p k q", k=KT), ACT.Copy).then_inc(ring_hi, 1)
                else:
                    nc.scalar.activation(oth[:, h], bank[:, 0:S], ACT.Identity, bias=bkv_s[:, 1, h:h + 1])\
                        .then_inc(ring_hi, 1)

            def exps(b, h):
                for t in range(ST):
                    act.wait_ge(max_ready, (b * H + h) * ST + t + 1)
                    nc.scalar.activation(pr[:, h % 2, t, :], sim[t][:], ACT.Exp, bias=nmax[:, h % 2, t:t + 1],
                                         accum_out=rsum[:, h % 2, t:t + 1]).then_inc(exp_done, 1)

            for i in range(len(start)):
                high_half(sections["start"], i)
            exps(0, 0)

            def turn(order, b, prev, nxt):
                i = 0
                for h in range(H):
                    if h + 1 < H:
                        exps(b, h + 1)
                    elif nxt:
                        exps(b + 1, 0)
                    n = len(slot(h, prev, nxt))
                    for j in range(n):
                        high_half(order, i + j)
                        if j == 0 and h == H - 3 and nxt:
                            affine(b + 1)
                    i += n
            sections_of(act, turn)
            high_half(Order([("O", H - 1)], tail_first + len(turn_fills(True, False))), 0)

        @block.vector
        def _(dve):
            def take(s, value):
                dve.wait_ge(s, value)
                dve.sem_inc(took, 1)

            def layer_norm(b, k, src, dst, steps):
                for t in range(ST):
                    last = nc.vector.bn_stats(stats[:, k, t, :], src[:, t, :])
                last.then_inc(dve_step, 1)
                take(dve_step, steps + 1)
                for t in range(ST):
                    last = nc.vector.bn_aggr(mv[:, k, t, :], stats[:, k, t, :])
                last.then_inc(var_ready, 1)
                dve.wait_ge(rstd_ready, b * 3 + k + 1)
                for t in range(ST):
                    last = nc.vector.tensor_scalar(dst[:, t, :], src[:, t, :], mv[:, k, t, 0:1],
                                                   rstd[:, k, t:t + 1], ALU.subtract, ALU.mult)
                last.then_inc(ln_ready, 1)

            def kv_halves(b):
                for k in range(2):
                    dve.wait_ge(aff_ready, (b * 2 + k) * DC + DC)
                    nc.vector.tensor_copy(kvh[:, :, k * S:(k + 1) * S], aff[:, k]).then_inc(kv_hi, 1)
                    dve.wait_ge(kv_hi, b * 2 + k + 1)
                    nc.vector.tensor_tensor(kvl[:, :, k * S:(k + 1) * S], aff[:, k],
                                            f32(kvh[:, :, k * S:(k + 1) * S]), ALU.subtract).then_inc(kv_ready, 1)

            def norms(b, k):
                if k == 0:
                    dve.wait_ge(in_c, b * 16 + 16)
                    layer_norm(b, 0, c_in, c_ln, b * 3)
                elif k == 1:
                    dve.wait_ge(in_x, b * 16 + 16)
                    layer_norm(b, 1, x_in, x_ln, b * 3 + 1)
                else:
                    dve.wait_ge(ln_ready, b * 3 + 2)
                    layer_norm(b, 2, x_ln, x_ln2, b * 3 + 2)

            for k in range(3):
                norms(0, k)
            for c in range(DC):
                dve.wait_ge(w_hi, c + 1)
                nc.vector.tensor_tensor(wkvl[:, c], stage_kv[:, c], f32(wkvh[:, c]), ALU.subtract).then_inc(w_lo, 1)
            kv_halves(0)
            dve.wait_ge(w_hi, DC + 2)
            nc.vector.scalar_tensor_tensor(wql[:].rearrange("p c n -> p (c n)"),
                                           stage_q[:].rearrange("p c n -> p (c n)"), QSCALE,
                                           f32(wqh[:]).rearrange("p c n -> p (c n)"), ALU.mult, ALU.subtract)\
                .then_inc(w_lo, 1)
            dve.wait_ge(w_hi, DC + 3)
            nc.vector.tensor_tensor(wol[:], stage_o[:], f32(woh[:]), ALU.subtract).then_inc(w_lo, 1)

            def low_half(order, i):
                name = order.names[i]
                bank = ring[order.bank(i, RING)]
                dve.wait_ge(ring_hi, order.at(i) + 1)
                h = name[1]
                if name[0] == "K":
                    nc.vector.scalar_tensor_tensor(ktl[:, h % 2], bank[:], bkv_s[:, 0, h:h + 1], f32(kth[:, h % 2]),
                                                   ALU.add, ALU.subtract).then_inc(ring_lo, 1)
                elif name[0] == "Q":
                    for j in range(2):
                        last = nc.vector.scalar_tensor_tensor(qtl[:, h % 2, j], bank[:, j * S:(j + 1) * S],
                                                              bq_s[:, 2 * h + j:2 * h + j + 1],
                                                              f32(qth[:, h % 2, j]), ALU.add, ALU.subtract)
                    last.then_inc(ring_lo, 1)
                elif name[0] == "V":
                    cols = slice(h // KT * HALF, (h // KT + 1) * HALF)
                    nc.vector.tensor_tensor(vl[:, h % KT, cols], bank[:], f32(vh[:, h % KT, cols]),
                                            ALU.subtract).then_inc(ring_lo, 1)
                elif name[0] == "T":
                    cols = slice(name[2] * P, (name[2] + 1) * P)
                    nc.vector.tensor_tensor(ptl[:, :, cols], bank[:].rearrange("p (k q) -> p k q", k=KT),
                                            f32(pth[:, :, cols]), ALU.subtract).then_inc(ring_lo, 1)
                else:
                    nc.vector.scalar_tensor_tensor(otl[:, h], bank[:, 0:S], bkv_s[:, 1, h:h + 1], f32(oth[:, h]),
                                                   ALU.add, ALU.subtract).then_inc(ring_lo, 1)

            def maxima(b, h):
                for t in range(ST):
                    dve.wait_ge(sim_full, (b * H + h) * ST + t + 1)
                    nc.vector.tensor_reduce(nmax[:, h % 2, t:t + 1], sim[t][:], AX.X, ALU.max, negate=True)\
                        .then_inc(max_ready, 1)

            def inverses(b, h, early):
                for t in range(ST):
                    n = (b * H + h) * ST + t + 1
                    dve.wait_ge(exp_done, n)
                    if not early:
                        dve.wait_ge(prob_ready, n - 2 * ST)
                    nc.vector.reciprocal(rinv[:, h % 2, t:t + 1], rsum[:, h % 2, t:t + 1]).then_inc(inv_ready, 1)

            def residual(b):
                dve.wait_ge(wo_full, b + 1)
                dve.wait_ge(res_ready, b + 1)
                if not isinstance(b, int) or b > 0:
                    dve.wait_ge(x1_out, b * 16)
                nc.vector.tensor_tensor(x_out[:].rearrange("p t d -> p (t d)"), ps_x[:],
                                        x_res[:].rearrange("p t d -> p (t d)"), ALU.add).then_inc(x1_ready, 1)

            for i in range(len(start)):
                low_half(sections["start"], i)
            maxima(0, 0)
            inverses(0, 0, True)

            def turn(order, b, prev, nxt):
                i = 0
                for h in range(H):
                    if h + 1 < H:
                        maxima(b, h + 1)
                    elif nxt:
                        maxima(b + 1, 0)
                    n = len(slot(h, prev, nxt))
                    for j in range(n):
                        if j == n - 2:
                            if h + 1 < H:
                                inverses(b, h + 1, not prev and h == 0)
                            elif nxt:
                                inverses(b + 1, 0, False)
                        low_half(order, i + j)
                        if j == 0 and h == H - 3 and nxt:
                            kv_halves(b + 1)
                        if j == 1 and h == 1 and prev:
                            residual(b - 1)
                    if nxt and h in (2, 3, 4):
                        norms(b + 1, h - 2)
                    i += n
            sections_of(dve, turn)
            low_half(Order([("O", H - 1)], tail_first + len(turn_fills(True, False))), 0)
            residual(B - 1)

        @block.tensor
        def _(pe):
            def product(out, parts, left_h, left_l, right_h, right_l):
                for n, part in enumerate(parts):
                    lh, ll, rh, rl = left_h(part), left_l(part), right_h(part), right_l(part)
                    nc.tensor.matmul(out, lh, rh, start=(n == 0), stop=False)
                    nc.tensor.matmul(out, lh, rl, start=False, stop=False)
                    last = nc.tensor.matmul(out, ll, rh, start=False, stop=(n == len(parts) - 1))
                return last

            def transposes(b):
                for k, (ln, ps) in enumerate(((c_ln, 0), (x_ln2, 1))):
                    pe.wait_ge(ln_ready, b * 3 + (1 if k == 0 else 3))
                    for c in range(DC):
                        for t in range(ST):
                            out = ps_c[:, c, t * P:(t + 1) * P] if k == 0 else \
                                ps_x[:, c * S + t * P:c * S + (t + 1) * P]
                            last = nc.tensor.transpose(out, ln[:, t, c * P:(c + 1) * P], ident[:])
                    last.then_inc(lnT_ready, 1)

            def scores(b, h, order, i):
                pe.wait_ge(ring_lo, order.done(("K", h), i))
                pe.wait_ge(ring_lo, order.done(("Q", h // 2), i))
                for t in range(ST):
                    if not (isinstance(b, int) and b == 0 and h == 0):
                        pe.wait_ge(exp_done, (b * H + h) * ST + t + 1 - ST)
                    q = slice(t * P, (t + 1) * P)
                    product(sim[t][:], [0], lambda _: qth[:, h // 2 % 2, h % 2, q], lambda _: qtl[:, h // 2 % 2, h % 2, q],
                            lambda _: kth[:, h % 2], lambda _: ktl[:, h % 2]).then_inc(sim_full, 1)

            def fill(order, i, b):
                name = order.names[i]
                bank = ring[order.bank(i, RING)]
                h = name[1]
                if order.turn is not None or order.first + i >= RING:
                    pe.wait_ge(ring_lo, order.at(i) + 1 - RING)
                if name[0] == "K":
                    cols = slice(h * DH, (h + 1) * DH)
                    last = product(bank[:], range(DC), lambda c: wkvh[:, c, cols], lambda c: wkvl[:, c, cols],
                                   lambda c: kvh[:, c, :], lambda c: kvl[:, c, :])
                elif name[0] == "Q":
                    for j in range(2):
                        cols = slice((2 * h + j) * DH, (2 * h + j + 1) * DH)
                        last = product(bank[:, j * S:(j + 1) * S], range(DC), lambda c: wqh[:, c, cols],
                                       lambda c: wql[:, c, cols], lambda c: kvh[:, c, S:], lambda c: kvl[:, c, S:])
                elif name[0] == "V":
                    rows = slice(h % KT * P, (h % KT + 1) * P)
                    cols = slice(INNER + h // KT * HALF, INNER + (h // KT + 1) * HALF)
                    last = product(bank[:], range(DC), lambda c: kvh[:, c, rows], lambda c: kvl[:, c, rows],
                                   lambda c: wkvh[:, c, cols], lambda c: wkvl[:, c, cols])
                elif name[0] == "T":
                    t = name[2]
                    pe.wait_ge(prob_ready, (b * H + h) * ST + t + 1)
                    for k in range(KT):
                        last = nc.tensor.transpose(bank[:, k * P:(k + 1) * P], pr[:, h % 2, t, k * P:(k + 1) * P],
                                                   ident[:])
                else:
                    pe.wait_ge(ring_lo, order.done(("T", h, ST - 1), i))
                    cols = slice(h * DH, (h + 1) * DH)
                    last = product(bank[:, 0:S], range(KT), lambda k: vh[:, k, cols], lambda k: vl[:, k, cols],
                                   lambda k: pth[:, k, :], lambda k: ptl[:, k, :])
                last.then_inc(ring_full, 1)

            def project_out(b, order, i):
                pe.wait_ge(ring_lo, order.done(("O", H - 1), i))
                for t in range(ST):
                    q = slice(t * P, (t + 1) * P)
                    last = product(ps_x[:, t * D:(t + 1) * D], range(H), lambda h: oth[:, h, q],
                                   lambda h: otl[:, h, q], lambda h: woh[:, h], lambda h: wol[:, h])
                last.then_inc(wo_full, 1)

            pe.wait_ge(consts, 1)
            transposes(0)
            pe.wait_ge(w_lo, DC + 2)
            pe.wait_ge(kv_ready, 2)
            for i in range(len(start)):
                fill(sections["start"], i, 0)
                if start[i] == ("K", 1):
                    scores(0, 0, sections["start"], i)

            def turn(order, b, prev, nxt):
                i = 0
                for h in range(H):
                    if h + 1 < H:
                        scores(b, h + 1, order, i)
                    elif nxt:
                        scores(b + 1, 0, order, i)
                    n = len(slot(h, prev, nxt))
                    for j in range(n):
                        if nxt and h == H - 2 and j == 0:
                            pe.wait_ge(kv_ready, b * 2 + 4)
                        if h == 1 and j == 1 and prev:
                            project_out(b - 1, order, i + j)
                        fill(order, i + j, b)
                        if j == 0 and h == H - 3 and nxt:
                            if prev:
                                pe.wait_ge(x1_ready, b)
                            transposes(b + 1)
                    i += n
            sections_of(pe, turn)
            end = Order([("O", H - 1)], tail_first + len(turn_fills(True, False)),
                        Order(turn_fills(True, False), 0))
            fill(end, 0, B - 1)
            project_out(B - 1, end, 1)


def ffn_attention_experts(nc, x1, ctxT, out, lora, W1T, b1, W2T, b2, scale, WqT, bq, WkT, bk, WvT, bv, Wg, Wu, Wd, Wr, temp):
    HID = W1T.shape[1]
    HC = HID // P
    E = Wg.shape[0]
    NL = 4
    A4 = D // NL
    GOLDEN_CENTER = 1.0 / 2.718281828459045
    GOLDEN_LOWER = 0.5 - 0.2876820724517809
    GOLDEN_UPPER = 0.5
    QSCALE = float(D) ** -0.5
    RING = 5

    def slot(e, nb, nn):
        if e == 0 and nb:
            return [("H", n) for n in range(HC // 2)], []
        if e == 1 and nb:
            return [("Y",)], [("K",), ("V",)]
        if e == 2 and nb:
            return [("B",)], [("Q",)]
        if e == 3 and nb:
            return [("S",)], ([("A",)] if nn else []) + [("T",)]
        if e == 4 and nb:
            return [("O",)], []
        if e == 6 and nb:
            return [("C",)], [("R",)]
        return [], []

    def turn_fills(nb, nn):
        return [f for e in range(E) for part in slot(e, nb, nn) for f in part]

    ONLY_DVE = ("Y", "O")

    class Fills(Order):
        def __init__(self, names, first, hi_first, before, step=0, hi_step=0, turn=None):
            super().__init__(names, first, before, step, turn)
            self.hi_first, self.hi_step = hi_first, hi_step

        def hi_at(self, i):
            n = self.hi_first + sum(f[0] not in ONLY_DVE for f in self.names[:i])
            return n if self.turn is None else n + self.turn * self.hi_step

    names_all = turn_fills(True, True)
    F = len(names_all)
    FH = sum(f[0] not in ONLY_DVE for f in names_all)
    assert F % RING == 0
    start = Fills([("A",)], 0, 0, None)

    ctx = ExitStack()
    with ctx:
        def sb(name, shape, dt=F32):
            return ctx.enter_context(nc.sbuf_tensor("b_" + name, shape, dt))

        def pb(name, shape):
            return ctx.enter_context(nc.psum_tensor("b_" + name, shape, F32))

        def sem(name):
            return ctx.enter_context(nc.semaphore("b_" + name))

        w1h, w1l = sb("w1h", [P, DC, HID], F32R), sb("w1l", [P, DC, HID], F32R)
        w2h, w2l = sb("w2h", [P, HC, D], F32R), sb("w2l", [P, HC, D], F32R)
        wqkvh, wqkvl = sb("wqkvh", [P, 3, DC, D], F32R), sb("wqkvl", [P, 3, DC, D], F32R)
        weh, wel = sb("weh", [P, 3, E, DC, D], F32R), sb("wel", [P, 3, E, DC, D], F32R)
        wrh, wrl = sb("wrh", [P, DC, E], F32R), sb("wrl", [P, DC, E], F32R)
        wr_raw = sb("wr_raw", [P, DC, E])
        stage = sb("stage", [P, 2, 2 * D])
        even = sb("even", [P, NL, D])
        b1_s, bq_raw, bq_s, bk_s = sb("b1_s", [P, HC]), sb("bq_raw", [P, DC]), sb("bq_s", [P, DC]), sb("bk_s", [P, DC])
        b2_b, bv_b = sb("b2_b", [P, D]), sb("bv_b", [P, D])
        lscale, tinv, thalf = sb("lscale", [P, 1]), sb("tinv", [P, 1]), sb("thalf", [P, 1])
        ident = sb("ident", [P, P])
        mhalf = sb("mhalf", [P, ST])
        index = sb("index", [P, E])
        x1_s, x2_s, acc = sb("x1_s", [P, ST, D]), sb("x2_s", [P, ST, D]), sb("acc", [P, ST, D])
        ln = sb("ln", [P, ST, D])
        stats, mv = sb("stats", [P, ST, 6]), sb("mv", [P, ST, 2])
        veps, rstd = sb("veps", [P, ST]), sb("rstd", [P, ST])
        xth, xtl = sb("xth", [P, DC, S], F32R), sb("xtl", [P, DC, S], F32R)
        xch, xcl = sb("xch", [P, DC, S], F32R), sb("xcl", [P, DC, S], F32R)
        odd = sb("odd", [P, DC, 2 * NL])
        hh, hl = sb("hh", [P, HC, S], F32R), sb("hl", [P, HC, S], F32R)
        ct_raw = sb("ct_raw", [P, DC, S])
        cth, ctl = sb("cth", [P, DC, S], F32R), sb("ctl", [P, DC, S], F32R)
        pr = sb("pr", [P, ST, S])
        lora_t = pr
        gel = [sb("gel", [P, ST * S])[:], pr[:].rearrange("p t s -> p (t s)")]
        nmax, rsum, rinv = sb("nmax", [P, ST]), sb("rsum", [P, ST]), sb("rinv", [P, ST])
        act_e = sb("act_e", [P, 2, 2 * S])
        heh, hel = sb("heh", [P, 2, 2, S], F32R), sb("hel", [P, 2, 2, S], F32R)
        th, sig, dist, near, wz, fb = (sb(n, [P, ST, E]) for n in ("th", "sig", "dist", "near", "wz", "fb"))
        top, mask, wts = (sb(n, [P, ST, E]) for n in ("top", "mask", "wts"))
        top_at = sb("top_at", [P, ST, E], mybir.dt.uint32)
        top_f = sb("top_f", [P, ST, 2])
        wsum, fsum, none_in, some_in = (sb(n, [P, ST]) for n in ("wsum", "fsum", "none_in", "some_in"))
        Q, K, V, PT = 0, 2, 4, 6

        ring = [pb(f"ring{i}", [P, 512]) for i in range(RING)]
        ps_g, ps_u, ps_d = pb("ps_g", [P, 512]), pb("ps_u", [P, 512]), pb("ps_d", [P, 512])

        small_in = sem("small_in")
        stage_in = [sem(f"stage_in{j}") for j in range(2)]
        stage_hi, stage_lo, stage_sum = sem("stage_hi"), sem("stage_lo"), sem("stage_sum")
        even_in, even_used, lora_out = sem("even_in"), sem("even_used"), sem("lora_out")
        consts, w_ready = sem("consts"), sem("w_ready")
        ring_full, ring_hi, ring_lo = sem("ring_full"), sem("ring_hi"), sem("ring_lo")
        x1_in, x1_biased, x2_ready, x2_biased, x3_ready = (
            sem(n) for n in ("x1_in", "x1_biased", "x2_ready", "x2_biased", "x3_ready"))
        ct_in, ct_hi, ct_lo = sem("ct_in"), sem("ct_hi"), sem("ct_lo")
        stats_ready, var_ready, rstd_ready, ln_ready = (
            sem(n) for n in ("stats_ready", "var_ready", "rstd_ready", "ln_ready"))
        odd_ready = sem("odd_ready")
        gel_ready, max_ready = sem("gel_ready"), sem("max_ready")
        gate_full, up_full, silu_done, he_ready, he_hi, he_lo, down_full, acc_ready = (
            sem(n) for n in ("gate_full", "up_full", "silu_done", "he_ready", "he_hi", "he_lo", "down_full", "acc_ready"))
        dist_ready, exps_ready, wts_ready = sem("dist_ready"), sem("exps_ready"), sem("wts_ready")
        route_step = sem("route_step")
        pool_step, took = sem("pool_step"), sem("took")
        out_done = sem("out_done")

        def sections_of(eng, body):
            first = Fills(names_all, 1, 1, start)
            body(first, 0, False, True, True)
            with eng.Fori(1, B - 1) as t:
                body(Fills(names_all, 1, 1, first, F, FH, t), t, True, True, True)
            loop = Fills(names_all, 0, 0, None)
            last = Fills(turn_fills(True, False), 1 + F * (B - 1), 1 + FH * (B - 1), loop)
            body(last, B - 1, True, True, False)
            body(Fills([], 0, 0, last), B, True, False, False)

        def ln_no(t, which):
            if isinstance(t, int) and t == B - 1:
                return 1 + 3 * t + {"B": 0, "C": 1}[which]
            return 1 + t * 3 + {"B": 0, "A": 1, "C": 2}[which]

        CHUNKS = 8
        PIECES = {4: (0, 1, 2), 5: (3, 4, 5), 6: (6, 7)}
        WARM = 3 * (E + 1)

        def piece_in(n, k):
            return ((WARM + k % 2) // 2 + n * (CHUNKS // 2) + k // 2 + 1) * 16

        x1_t = x1.rearrange("b (t p) d -> b p t d", p=P)
        out_t = out.rearrange("b (t p) d -> b p t d", p=P)
        ct_t = ctxT.rearrange("b (c p) s -> b p c s", p=P)

        block = ctx.enter_context(nc.Block())

        @block.sync
        def _(sp):
            def take(s, value):
                sp.wait_ge(s, value)
                sp.sem_inc(took, 1)

            def weights_of(n, first):
                for k in range(CHUNKS):
                    take(stage_lo, n * CHUNKS + WARM + k - 1)
                    if k < CHUNKS // 2:
                        src = W1T[k // 2 * P:(k // 2 + 1) * P, k % 2 * 2 * D:(k % 2 + 1) * 2 * D]
                        dst = stage[:, k % 2, :]
                    else:
                        g = k - CHUNKS // 2
                        src = W2T[g * 2 * P:(g + 1) * 2 * P, :].rearrange("(c p) d -> p c d", p=P)
                        dst = stage[:, k % 2, :].rearrange("p (c d) -> p c d", c=2)
                    sp.dma_start(dst, src).then_inc(stage_in[k % 2], 16)
                    if k == 0:
                        take(lora_out, n * 16 + 16)
                        if not first:
                            take(even_used, n * 2)
                        sp.dma_start(even[:], lora[n, 0:2 * NL:2, :].unsqueeze(0).to_broadcast([P, NL, D]))\
                            .then_inc(even_in, 16)
                    if k == CHUNKS // 2:
                        take(even_used, n * 2 + 1)
                        sp.dma_start(even[:], lora[n, 2 * NL:4 * NL:2, :].unsqueeze(0).to_broadcast([P, NL, D]))\
                            .then_inc(even_in, 16)

            sp.dma_start(x1_s[:], x1_t[0]).then_inc(x1_in, 16)
            for dst, src in ((b1_s, b1), (bq_raw, bq), (bk_s, bk)):
                sp.dma_start(dst[:], src).then_inc(small_in, 16)
            for dst, src in ((b2_b, b2), (bv_b, bv)):
                sp.dma_start(dst[:], src.to_broadcast([P, D])).then_inc(small_in, 16)
            sp.dma_start(lscale[:], scale.to_broadcast([P, 1])).then_inc(small_in, 16)
            sp.dma_start(tinv[:], temp.to_broadcast([P, 1])).then_inc(small_in, 16)
            sp.dma_start(wr_raw[:], Wr.rearrange("(c p) e -> p c e", p=P)).then_inc(small_in, 16)
            sp.dma_start(ct_raw[:], ct_t[0]).then_inc(ct_in, 16)
            for k in range(WARM):
                if k >= 2:
                    sp.wait_ge(stage_lo, k - 1)
                src = (WqT, WkT, WvT)[k] if k < 3 else (Wg, Wu, Wd)[k % 3][k // 3 - 1]
                sp.dma_start(stage[:, (k + 1) % 2, :].rearrange("p (c d) -> p c d", c=DC),
                             src.rearrange("(c p) d -> p c d", p=P)).then_inc(stage_in[(k + 1) % 2], 16)
            sp.wait_ge(ln_ready, 1)
            sp.dma_start(lora[0], ln[1:1 + 4 * NL, 0, :]).then_inc(lora_out, 16)
            weights_of(0, True)

            def turn(fills, t, experts, nb, nn):
                if experts and nb:
                    take(ct_lo, t)
                    sp.dma_start(ct_raw[:], ct_t[t]).then_inc(ct_in, 16)
                if nn:
                    take(x2_ready, t + 1)
                    sp.dma_start(x1_s[:], x1_t[t + 1]).then_inc(x1_in, 16)
                    take(ln_ready, ln_no(t, "A") + 1)
                    sp.dma_start(lora[t + 1], ln[1:1 + 4 * NL, 0, :]).then_inc(lora_out, 16)
                    weights_of(t + 1, False)
                if experts:
                    take(acc_ready, t * E)
                    sp.dma_start(out_t[t - 1], acc[:]).then_inc(out_done, 16)
            sections_of(sp, turn)
            sp.wait_ge(out_done, 16 * B)

        @block.gpsimd
        def _(pool):
            def take(s, value):
                pool.wait_ge(s, value)
                pool.sem_inc(took, 1)

            nc.gpsimd.memset(ident[:], 0.0).then_inc(pool_step, 1)
            nc.gpsimd.memset(mhalf[:], -0.5).then_inc(pool_step, 1)
            pool.wait_ge(pool_step, 2)
            nc.gpsimd.affine_select(out=ident[:], in_=ident[:], compare_op=ALU.not_equal, fill=1.0, base=0,
                                    pattern=[[-1, P]], channel_multiplier=1).then_inc(consts, 1)
            for e in range(E):
                last = nc.gpsimd.memset(index[:, e:e + 1], float(e))
            last.then_inc(consts, 1)
            pool.wait_ge(consts, 2)
            def rstd_of(n, base):
                take(var_ready, n + 1)
                nc.gpsimd.tensor_scalar(veps[:], mv[:, :, 1], EPS, 1.0, ALU.add, ALU.mult).then_inc(pool_step, 1)
                pool.wait_ge(pool_step, base + 1)
                nc.gpsimd.tensor_tensor(rstd[:], veps[:], mhalf[:], ALU.pow).then_inc(rstd_ready, 1)

            def bias_x1(n, l):
                pool.wait_ge(ln_ready, l + 1)
                nc.gpsimd.tensor_tensor(x1_s[:], x1_s[:], b2_b[:].unsqueeze(1).to_broadcast([P, ST, D]), ALU.add)\
                    .then_inc(x1_biased, 1)

            def low_rank_2(n, base):
                for g in range(NL):
                    k = NL + g
                    pool.wait_ge(stage_in[k % 2], piece_in(n, k))
                    if g == 0:
                        pool.wait_ge(even_in, n * 32 + 32)
                        pool.wait_ge(odd_ready, n + 1)
                    for c in range(DC):
                        last = nc.gpsimd.tensor_tensor(
                            lora_t[:, c, :].rearrange("p (i a) -> p i a", i=NL),
                            even[:].rearrange("p i (a m) -> p i a m", m=4)[:, :, :, g],
                            odd[:, c, NL:].unsqueeze(2).to_broadcast([P, NL, A4]), ALU.mult)
                    last.then_inc(pool_step, 1)
                    pool.wait_ge(pool_step, base + g + 1)
                    nc.gpsimd.tensor_tensor(stage[:, k % 2, :], stage[:, k % 2, :],
                                            lora_t[:].rearrange("p c d -> p (c d)"), ALU.add).then_inc(stage_sum, 1)
                    pool.wait_ge(stage_sum, n * 2 * NL + NL + g + 1)
                pool.sem_inc(even_used, 1)

            rstd_of(0, 2)
            pool.wait_ge(small_in, 16 * 8)
            bias_x1(0, 0)
            low_rank_2(0, 3)
            START = 3 + NL

            def turn(fills, t, experts, nb, nn):
                base = START + t * (3 + NL)
                if nb:
                    rstd_of(ln_no(t, "B"), base)
                    take(ln_ready, ln_no(t, "B") + 1)
                    nc.gpsimd.tensor_tensor(x2_s[:], x2_s[:], bv_b[:].unsqueeze(1).to_broadcast([P, ST, D]),
                                            ALU.add).then_inc(x2_biased, 1)
                if nn:
                    rstd_of(ln_no(t, "A"), base + 1)
                    bias_x1(t + 1, ln_no(t, "A"))
                if nb:
                    rstd_of(ln_no(t, "C"), base + (2 if nn else 1))
                if nn:
                    low_rank_2(t + 1, base + 3)
            sections_of(pool, turn)

        @block.scalar
        def _(act):
            act.wait_ge(small_in, 16 * 8)
            nc.scalar.activation(bq_s[:], bq_raw[:], ACT.Copy, scale=QSCALE).then_inc(stage_hi, 1)
            nc.scalar.activation(wrh[:], wr_raw[:], ACT.Copy).then_inc(stage_hi, 1)
            HI0 = 2
            for k in range(WARM):
                act.wait_ge(stage_in[(k + 1) % 2], (k // 2 + 1) * 16)
                dst = wqkvh[:, k] if k < 3 else weh[:, k % 3, k // 3 - 1]
                nc.scalar.activation(dst.rearrange("p c d -> p (c d)"), stage[:, (k + 1) % 2, :], ACT.Copy,
                                     scale=QSCALE if k == 0 else 1.0).then_inc(stage_hi, 1)

            def weights_high(n, k):
                act.wait_ge(stage_sum, n * 2 * NL + k + 1)
                if k < NL:
                    dst = w1h[:, k // 2, k % 2 * 2 * D:(k % 2 + 1) * 2 * D]
                else:
                    dst = w2h[:, 2 * (k - NL):2 * (k - NL) + 2, :].rearrange("p c d -> p (c d)")
                nc.scalar.activation(dst, stage[:, k % 2, :], ACT.Copy).then_inc(stage_hi, 1)

            def context_high(t):
                act.wait_ge(ct_in, t * 16 + 16)
                nc.scalar.activation(cth[:], ct_raw[:], ACT.Copy).then_inc(ct_hi, 1)

            def silu(i, e):
                act.wait_ge(gate_full, i * E + e + 1)
                nc.scalar.activation(act_e[:, e % 2, :], ps_g[:], ACT.Silu).then_inc(silu_done, 1)

            def hidden_high(i, e):
                act.wait_ge(he_ready, i * E + e + 1)
                nc.scalar.activation(heh[:, e % 2].rearrange("p c s -> p (c s)"), act_e[:, e % 2, :], ACT.Copy)\
                    .then_inc(he_hi, 1)

            def high(fills, i, t):
                name = fills.names[i]
                kind = name[0]
                if kind in ONLY_DVE:
                    return
                bank = ring[fills.bank(i, RING)]
                cd = bank[:].rearrange("p (c d) -> p c d", c=2)
                if kind == "S":
                    act.wait_ge(max_ready, t + 1)
                    for k in range(ST):
                        last = nc.scalar.activation(pr[:, k, :], cd[:, k, :], ACT.Exp, bias=nmax[:, k:k + 1],
                                                    accum_out=rsum[:, k:k + 1])
                    last.then_inc(ring_hi, 1)
                    return
                act.wait_ge(ring_full, fills.at(i) + 1)
                if kind == "H":
                    n = name[1]
                    if n >= 2:
                        act.wait_ge(ring_lo, fills.at(i) + 1 - 2)
                    for k in range(2):
                        last = nc.scalar.activation(gel[n % 2][:, k * S:(k + 1) * S], cd[:, k, :], ACT.Gelu,
                                                    bias=b1_s[:, 2 * n + k:2 * n + k + 1])
                    last.then_inc(gel_ready, 1)
                    act.wait_ge(gel_ready, t * (HC // 2) + n + 1)
                    nc.scalar.activation(hh[:, 2 * n:2 * n + 2, :].rearrange("p c s -> p (c s)"), gel[n % 2],
                                         ACT.Copy).then_inc(ring_hi, 1)
                elif kind in "QK":
                    at, bias = (Q, bq_s) if kind == "Q" else (K, bk_s)
                    for k in range(DC):
                        last = nc.scalar.activation(hh[:, at + k, :], cd[:, k, :], ACT.Identity, bias=bias[:, k:k + 1])
                    last.then_inc(ring_hi, 1)
                elif kind == "R":
                    nc.scalar.activation(th[:].rearrange("p t e -> p (t e)"), bank[:, 0:ST * E], ACT.Tanh,
                                         scale=thalf[:, 0:1]).then_inc(ring_hi, 1)
                else:
                    dst = {"A": xth[:], "B": xth[:], "C": xch[:], "V": hh[:, V:V + 2, :], "T": hh[:, PT:PT + 2, :]}[kind]
                    nc.scalar.activation(dst, cd, ACT.Copy).then_inc(ring_hi, 1)

            def routing_exps(t):
                act.wait_ge(dist_ready, t + 1)
                nc.scalar.activation(wz[:], dist[:], ACT.Exp, scale=-1.0 / 0.1).then_inc(exps_ready, 1)
                nc.scalar.activation(fb[:], dist[:], ACT.Exp, scale=-1.0 / 0.3).then_inc(exps_ready, 1)

            high(start, 0, 0)
            for k in range(CHUNKS):
                weights_high(0, k)

            def turn(fills, t, experts, nb, nn):
                i = 0
                for e in range(E):
                    if e + 1 < E and experts:
                        silu(t - 1, e + 1)
                    elif e + 1 == E and nb:
                        silu(t, 0)
                    if e == 0 and nb:
                        context_high(t)
                    before, after = slot(e, nb, nn)
                    for _ in before:
                        high(fills, i, t)
                        i += 1
                    if e + 1 < E and experts:
                        hidden_high(t - 1, e + 1)
                    elif e + 1 == E and nb:
                        hidden_high(t, 0)
                    for _ in after:
                        high(fills, i, t)
                        i += 1
                    if e == 6 and nb:
                        routing_exps(t)
                    if nn:
                        for k in PIECES.get(e, ()):
                            weights_high(t + 1, k)
            sections_of(act, turn)

        @block.vector
        def _(dve):
            def take(s, value):
                dve.wait_ge(s, value)
                dve.sem_inc(took, 1)

            def layer_norm(n, src):
                for k in range(ST):
                    last = nc.vector.bn_stats(stats[:, k, :], src[:, k, :])
                last.then_inc(stats_ready, 1)
                take(stats_ready, n + 1)
                for k in range(ST):
                    last = nc.vector.bn_aggr(mv[:, k, :], stats[:, k, :])
                last.then_inc(var_ready, 1)
                dve.wait_ge(rstd_ready, n + 1)
                for k in range(ST):
                    last = nc.vector.tensor_scalar(ln[:, k, :], src[:, k, :], mv[:, k, 0:1], rstd[:, k:k + 1],
                                                   ALU.subtract, ALU.mult)
                last.then_inc(ln_ready, 1)

            def weights_low(n, k):
                if k < NL:
                    dve.wait_ge(stage_in[k % 2], piece_in(n, k))
                    if k == 0:
                        dve.wait_ge(even_in, n * 32 + 16)
                        dve.wait_ge(odd_ready, n + 1)
                    for j in range(2):
                        i = k % 2 * 2 + j
                        part = stage[:, k % 2, j * D:(j + 1) * D]
                        last = nc.vector.scalar_tensor_tensor(part, even[:, i, :], odd[:, k // 2, i:i + 1], part,
                                                              ALU.mult, ALU.add)
                    last.then_inc(stage_sum, 1)
                    if k == NL - 1:
                        dve.wait_ge(stage_sum, n * 2 * NL + NL)
                        dve.sem_inc(even_used, 1)
                    dh, dl = (w[:, k // 2, k % 2 * 2 * D:(k % 2 + 1) * 2 * D] for w in (w1h, w1l))
                else:
                    dh, dl = (w[:, 2 * (k - NL):2 * (k - NL) + 2, :].rearrange("p c d -> p (c d)") for w in (w2h, w2l))
                dve.wait_ge(stage_hi, n * CHUNKS + 2 + WARM + k + 1)
                nc.vector.tensor_tensor(dl, stage[:, k % 2, :], f32(dh), ALU.subtract).then_inc(stage_lo, 1)

            def context_low(t):
                dve.wait_ge(ct_hi, t + 1)
                nc.vector.tensor_tensor(ctl[:], ct_raw[:], f32(cth[:]), ALU.subtract).then_inc(ct_lo, 1)

            def hidden(i, e):
                dve.wait_ge(silu_done, i * E + e + 1)
                dve.wait_ge(up_full, i * E + e + 1)
                nc.vector.tensor_tensor(act_e[:, e % 2, :], act_e[:, e % 2, :], ps_u[:], ALU.mult).then_inc(he_ready, 1)

            def hidden_low(i, e):
                dve.wait_ge(he_hi, i * E + e + 1)
                nc.vector.tensor_tensor(hel[:, e % 2].rearrange("p c s -> p (c s)"), act_e[:, e % 2, :],
                                        f32(heh[:, e % 2]).rearrange("p c s -> p (c s)"), ALU.subtract)\
                    .then_inc(he_lo, 1)

            def weigh(i, e):
                dve.wait_ge(down_full, i * E + e + 1)
                if e == 0:
                    dve.wait_ge(wts_ready, i + 1)
                    dve.wait_ge(out_done, i * 16)
                else:
                    dve.wait_ge(acc_ready, i * E + e)
                for k in range(ST):
                    last = nc.vector.scalar_tensor_tensor(acc[:, k, :], ps_d[:, k * D:(k + 1) * D],
                                                          wts[:, k, e:e + 1], (x2_s if e == 0 else acc)[:, k, :],
                                                          ALU.mult, ALU.add)
                last.then_inc(acc_ready, 1)

            def low(fills, i, t, experts=False):
                name = fills.names[i]
                kind = name[0]
                bank = ring[fills.bank(i, RING)]
                cd = bank[:].rearrange("p (c d) -> p c d", c=2)
                if kind == "Y":
                    dve.wait_ge(ring_full, fills.at(i) + 1)
                    dve.wait_ge(x1_biased, t + 1)
                    if experts:
                        dve.wait_ge(acc_ready, (t - 1) * E + 1)
                    nc.vector.tensor_tensor(x2_s[:], cd, x1_s[:], ALU.add).then_inc(x2_ready, 1)
                    dve.wait_ge(x2_ready, t + 1)
                    dve.sem_inc(ring_lo, 1)
                    return
                if kind == "O":
                    dve.wait_ge(ring_full, fills.at(i) + 1)
                    dve.wait_ge(x2_biased, t + 1)
                    for k in range(ST):
                        last = nc.vector.scalar_tensor_tensor(x2_s[:, k, :], cd[:, k, :], rinv[:, k:k + 1],
                                                              x2_s[:, k, :], ALU.mult, ALU.add)
                    last.then_inc(x3_ready, 1)
                    dve.wait_ge(x3_ready, t + 1)
                    dve.sem_inc(ring_lo, 1)
                    return
                if kind == "S":
                    dve.wait_ge(ring_full, fills.at(i) + 1)
                    nc.vector.tensor_reduce(nmax[:], cd, AX.X, ALU.max, negate=True).then_inc(max_ready, 1)
                    dve.wait_ge(ring_hi, fills.hi_at(i) + 1)
                    nc.vector.reciprocal(rinv[:], rsum[:]).then_inc(ring_lo, 1)
                    return
                dve.wait_ge(ring_hi, fills.hi_at(i) + 1)
                if kind == "H":
                    n = name[1]
                    nc.vector.tensor_tensor(hl[:, 2 * n:2 * n + 2, :].rearrange("p c s -> p (c s)"), gel[n % 2],
                                            f32(hh[:, 2 * n:2 * n + 2, :]).rearrange("p c s -> p (c s)"),
                                            ALU.subtract).then_inc(ring_lo, 1)
                elif kind in "QK":
                    at, bias = (Q, bq_s) if kind == "Q" else (K, bk_s)
                    for k in range(DC):
                        last = nc.vector.scalar_tensor_tensor(hl[:, at + k, :], cd[:, k, :], bias[:, k:k + 1],
                                                              f32(hh[:, at + k, :]), ALU.add, ALU.subtract)
                    last.then_inc(ring_lo, 1)
                elif kind == "R":
                    nc.vector.tensor_scalar(sig[:], th[:], 0.5, 0.5, ALU.mult, ALU.add).then_inc(ring_lo, 1)
                    dve.wait_ge(ring_lo, fills.at(i) + 1)
                    nc.vector.tensor_scalar(dist[:], sig[:], GOLDEN_CENTER, None, ALU.subtract)
                    nc.vector.tensor_scalar(near[:], sig[:], GOLDEN_LOWER, None, ALU.is_ge).then_inc(route_step, 1)
                    dve.wait_ge(route_step, t * (ROUTE + 1) + 1)
                    nc.vector.scalar_tensor_tensor(near[:], sig[:], GOLDEN_UPPER, near[:], ALU.is_le, ALU.mult)
                    nc.vector.scalar_tensor_tensor(dist[:], dist[:], -1.0, dist[:], ALU.mult, ALU.max)\
                        .then_inc(dist_ready, 1)
                else:
                    dh, dl = {"A": (xth[:], xtl[:]), "B": (xth[:], xtl[:]), "C": (xch[:], xcl[:]),
                              "V": (hh[:, V:V + 2, :], hl[:, V:V + 2, :]),
                              "T": (hh[:, PT:PT + 2, :], hl[:, PT:PT + 2, :])}[kind]
                    if kind == "A":
                        nc.vector.tensor_scalar(odd[:], cd[:, :, 2:2 + 4 * NL:2], lscale[:, 0:1], None, ALU.mult)\
                            .then_inc(odd_ready, 1)
                    nc.vector.tensor_tensor(dl, cd, f32(dh), ALU.subtract).then_inc(ring_lo, 1)

            ROUTE = 14

            def routing(t):
                n = [0]

                def stage_of(*run):
                    for ins in run:
                        last = ins()
                    last.then_inc(route_step, 1)
                    n[0] += 1
                    take(route_step, t * (ROUTE + 1) + 1 + n[0])

                v = nc.vector

                def wide(a):
                    return a[:].unsqueeze(2).to_broadcast([P, ST, E])

                take(exps_ready, t * 2 + 2)
                tiles = range(ST)
                stage_of(lambda: v.tensor_tensor(wz[:], wz[:], near[:], ALU.mult),
                         *[lambda k=k: v.max(top[:, k, :], fb[:, k, :]) for k in tiles])
                stage_of(lambda: v.reduce_sum(wsum[:], wz[:], AX.X),
                         *[lambda k=k: v.max_index(top_at[:, k, :], top[:, k, :], fb[:, k, :]) for k in tiles])
                stage_of(lambda: v.tensor_scalar(none_in[:], wsum[:], 1e-8, None, ALU.is_lt),
                         lambda: v.tensor_copy(top_f[:], top_at[:, :, 0:2]))
                stage_of(lambda: v.tensor_scalar(some_in[:], none_in[:], -1.0, 1.0, ALU.mult, ALU.add),
                         *[lambda k=k: v.tensor_scalar(mask[:, k, :], index[:], top_f[:, k, 0:1], None, ALU.is_equal)
                           for k in tiles])
                stage_of(*[lambda k=k: v.scalar_tensor_tensor(mask[:, k, :], index[:], top_f[:, k, 1:2],
                                                              mask[:, k, :], ALU.is_equal, ALU.add) for k in tiles])
                stage_of(lambda: v.tensor_tensor(fb[:], fb[:], mask[:], ALU.mult),
                         lambda: v.tensor_tensor(wz[:], wz[:], wide(some_in), ALU.mult))
                stage_of(lambda: v.reduce_sum(fsum[:], fb[:], AX.X))
                stage_of(lambda: v.tensor_scalar(fsum[:], fsum[:], 1e-8, None, ALU.max))
                stage_of(lambda: v.reciprocal(fsum[:], fsum[:]))
                stage_of(lambda: v.tensor_tensor(fsum[:], fsum[:], none_in[:], ALU.mult))
                stage_of(*[lambda k=k: v.scalar_tensor_tensor(wz[:, k, :], fb[:, k, :], fsum[:, k:k + 1], wz[:, k, :],
                                                              ALU.mult, ALU.add) for k in tiles])
                stage_of(lambda: v.reduce_sum(wsum[:], wz[:], AX.X))
                stage_of(lambda: v.tensor_scalar(wsum[:], wsum[:], 1e-8, None, ALU.max))
                stage_of(lambda: v.reciprocal(wsum[:], wsum[:]))
                assert n[0] == ROUTE
                v.tensor_tensor(wts[:], wz[:], wide(wsum), ALU.mult).then_inc(wts_ready, 1)

            dve.wait_ge(x1_in, 16)
            layer_norm(0, x1_s)
            dve.wait_ge(small_in, 16 * 8)
            nc.vector.reciprocal(tinv[:], tinv[:]).then_inc(w_ready, 1)
            dve.wait_ge(w_ready, 1)
            nc.vector.tensor_scalar(thalf[:], tinv[:], 0.5, None, ALU.mult).then_inc(w_ready, 1)
            dve.wait_ge(stage_hi, 2)
            nc.vector.tensor_tensor(wrl[:], wr_raw[:], f32(wrh[:]), ALU.subtract).then_inc(w_ready, 1)
            for k in range(WARM):
                dve.wait_ge(stage_hi, 2 + k + 1)
                dh, dl = (wqkvh[:, k], wqkvl[:, k]) if k < 3 else (weh[:, k % 3, k // 3 - 1], wel[:, k % 3, k // 3 - 1])
                dh, dl = f32(dh).rearrange("p c d -> p (c d)"), dl.rearrange("p c d -> p (c d)")
                if k == 0:
                    nc.vector.scalar_tensor_tensor(dl, stage[:, 1, :], QSCALE, dh, ALU.mult, ALU.subtract)\
                        .then_inc(stage_lo, 1)
                else:
                    nc.vector.tensor_tensor(dl, stage[:, (k + 1) % 2, :], dh, ALU.subtract).then_inc(stage_lo, 1)
            low(start, 0, 0)
            for k in range(CHUNKS):
                weights_low(0, k)

            def turn(fills, t, experts, nb, nn):
                i = 0
                for e in range(E):
                    if e == 0 and nb:
                        context_low(t)
                    if e + 1 < E and experts:
                        hidden(t - 1, e + 1)
                    elif e + 1 == E and nb:
                        hidden(t, 0)
                    before, after = slot(e, nb, nn)
                    for f in before:
                        low(fills, i, t, experts)
                        i += 1
                        if f[0] == "Y" and not experts:
                            dve.wait_ge(lora_out, 16)
                        if f[0] == "Y":
                            layer_norm(ln_no(t, "B"), x2_s)
                        if f[0] == "O" and nn:
                            dve.wait_ge(lora_out, t * 16 + 32)
                        if f[0] == "O":
                            layer_norm(ln_no(t, "C"), x2_s)
                    if e + 1 < E and experts:
                        hidden_low(t - 1, e + 1)
                    elif e + 1 == E and nb:
                        hidden_low(t, 0)
                    if experts:
                        weigh(t - 1, e)
                    for _ in after:
                        low(fills, i, t, experts)
                        i += 1
                    if e == 2 and nn:
                        dve.wait_ge(x1_in, t * 16 + 32)
                        layer_norm(ln_no(t, "A"), x1_s)
                    if nn:
                        for k in PIECES.get(e, ()):
                            weights_low(t + 1, k)
                    if e == E - 1 and nb:
                        routing(t)
            sections_of(dve, turn)

        @block.tensor
        def _(pe):
            def product(out, parts, left_h, left_l, right_h, right_l):
                for n, part in enumerate(parts):
                    lh, ll, rh, rl = left_h(part), left_l(part), right_h(part), right_l(part)
                    nc.tensor.matmul(out, lh, rh, start=(n == 0), stop=False)
                    nc.tensor.matmul(out, lh, rl, start=False, stop=False)
                    last = nc.tensor.matmul(out, ll, rh, start=False, stop=(n == len(parts) - 1))
                return last

            def fill(fills, i, t):
                name = fills.names[i]
                kind = name[0]
                bank = ring[fills.bank(i, RING)]
                cd = bank[:].rearrange("p (c d) -> p c d", c=2)
                if fills.turn is not None or fills.first + i >= RING:
                    pe.wait_ge(ring_lo, fills.at(i) + 1 - RING)
                if kind in "ABC":
                    pe.wait_ge(ln_ready, (0 if fills is start else ln_no(t, kind)) + 1)
                    for c in range(DC):
                        for k in range(ST):
                            last = nc.tensor.transpose(cd[:, c, k * P:(k + 1) * P], ln[:, k, c * P:(c + 1) * P], ident[:])
                elif kind == "H":
                    if name[1] == 0:
                        pe.wait_ge(stage_lo, t * CHUNKS + WARM + CHUNKS)
                        pe.wait_ge(ring_lo, fills.done(("A",), i))
                    for k in range(2):
                        cols = slice((2 * name[1] + k) * P, (2 * name[1] + k + 1) * P)
                        last = product(cd[:, k, :], range(DC), lambda c: w1h[:, c, cols], lambda c: w1l[:, c, cols],
                                       lambda c: xth[:, c, :], lambda c: xtl[:, c, :])
                elif kind == "Y":
                    pe.wait_ge(ring_lo, fills.done(("H", HC // 2 - 1), i))
                    for k in range(ST):
                        q = slice(k * P, (k + 1) * P)
                        last = product(cd[:, k, :], range(HC), lambda c: hh[:, c, q], lambda c: hl[:, c, q],
                                       lambda c: w2h[:, c, :], lambda c: w2l[:, c, :])
                elif kind in "QK":
                    w, (rh, rl) = (0, (xth, xtl)) if kind == "Q" else (1, (cth, ctl))
                    if kind == "Q":
                        pe.wait_ge(ring_lo, fills.done(("B",), i))
                    else:
                        pe.wait_ge(ct_lo, t + 1)
                    for k in range(DC):
                        cols = slice(k * P, (k + 1) * P)
                        last = product(cd[:, k, :], range(DC), lambda c: wqkvh[:, w, c, cols], lambda c: wqkvl[:, w, c, cols],
                                       lambda c: rh[:, c, :], lambda c: rl[:, c, :])
                elif kind == "V":
                    for k in range(ST):
                        q = slice(k * P, (k + 1) * P)
                        last = product(cd[:, k, :], range(DC), lambda c: cth[:, c, q], lambda c: ctl[:, c, q],
                                       lambda c: wqkvh[:, 2, c, :], lambda c: wqkvl[:, 2, c, :])
                elif kind == "S":
                    pe.wait_ge(ring_lo, fills.done(("Q",), i))
                    for k in range(ST):
                        q = slice(k * P, (k + 1) * P)
                        last = product(cd[:, k, :], range(DC), lambda c: hh[:, Q + c, q], lambda c: hl[:, Q + c, q],
                                       lambda c: hh[:, K + c, :], lambda c: hl[:, K + c, :])
                elif kind == "T":
                    pe.wait_ge(ring_lo, fills.done(("S",), i))
                    for k in range(ST):
                        for q in range(ST):
                            last = nc.tensor.transpose(cd[:, k, q * P:(q + 1) * P], pr[:, q, k * P:(k + 1) * P], ident[:])
                elif kind == "O":
                    pe.wait_ge(ring_lo, fills.done(("T",), i))
                    for k in range(ST):
                        q = slice(k * P, (k + 1) * P)
                        last = product(cd[:, k, :], range(ST), lambda c: hh[:, PT + c, q], lambda c: hl[:, PT + c, q],
                                       lambda c: hh[:, V + c, :], lambda c: hl[:, V + c, :])
                else:
                    pe.wait_ge(ring_lo, fills.done(("C",), i))
                    for k in range(ST):
                        q = slice(k * P, (k + 1) * P)
                        last = product(bank[:, k * E:(k + 1) * E], range(DC), lambda c: xch[:, c, q],
                                       lambda c: xcl[:, c, q], lambda c: wrh[:, c, :], lambda c: wrl[:, c, :])
                last.then_inc(ring_full, 1)

            def gate_up(i, e, first=False):
                for w, (ps, full) in enumerate(((ps_g, gate_full), (ps_u, up_full))):
                    if not first:
                        pe.wait_ge(silu_done if w == 0 else he_ready, i * E + e)
                    for k in range(2):
                        cols = slice(k * P, (k + 1) * P)
                        last = product(ps[:, k * S:(k + 1) * S], range(DC), lambda c: weh[:, w, e, c, cols],
                                       lambda c: wel[:, w, e, c, cols], lambda c: xch[:, c, :], lambda c: xcl[:, c, :])
                    last.then_inc(full, 1)

            def down(i, e):
                pe.wait_ge(he_lo, i * E + e + 1)
                pe.wait_ge(acc_ready, i * E + e)
                for k in range(ST):
                    q = slice(k * P, (k + 1) * P)
                    last = product(ps_d[:, k * D:(k + 1) * D], range(2), lambda c: heh[:, e % 2, c, q],
                                   lambda c: hel[:, e % 2, c, q], lambda c: weh[:, 2, e, c, :],
                                   lambda c: wel[:, 2, e, c, :])
                last.then_inc(down_full, 1)

            pe.wait_ge(consts, 2)
            fill(start, 0, 0)
            pe.wait_ge(w_ready, 3)

            def turn(fills, t, experts, nb, nn):
                i = 0
                for e in range(E):
                    if e + 1 < E and experts:
                        gate_up(t - 1, e + 1)
                    elif e + 1 == E and nb:
                        pe.wait_ge(ring_lo, fills.done(("C",), i))
                        gate_up(t, 0, first=not experts)
                    before, after = slot(e, nb, nn)
                    for _ in before:
                        fill(fills, i, t)
                        i += 1
                    if experts:
                        down(t - 1, e)
                    for _ in after:
                        fill(fills, i, t)
                        i += 1
            sections_of(pe, turn)


def program(nc, x, ctx_in, ctxT, a_args, b_args, out, x1, lora):
    latent_attention(nc, x, ctx_in, x1, *a_args)
    ffn_attention_experts(nc, x1, ctxT, out, lora, *b_args)


def kernel(x, ctx_1024, L0_xattn_gamma_media, L0_xattn_beta_media, L0_xattn_gamma_lat, L0_xattn_beta_lat, L0_xattn_Wq,
           L0_xattn_bq, L0_xattn_Wkv, L0_xattn_bkv, L0_xattn_Wo, L0_xattn_bo, L0_ffn_W1, L0_ffn_b1, L0_ffn_W2,
           L0_ffn_b2, L0_ffn_scale, L1_xattn_Wq_w, L1_xattn_Wq_b, L1_xattn_Wk_w, L1_xattn_Wk_b, L1_xattn_Wv_w,
           L1_xattn_Wv_b, L1_ffn_Wg, L1_ffn_Wu, L1_ffn_Wd, L1_ffn_Wr, L1_ffn_temperature):
    import numpy as np
    import concourse.bacc as bacc
    from concourse.bass_utils import run_bass_kernel_spmd

    def arr(a):
        return np.asarray(a)

    def cols(a):
        return arr(a).reshape(-1, P).T

    def row(a):
        return arr(a).reshape(1, -1)

    group_a = dict(
        g_media=cols(L0_xattn_gamma_media), b_media=cols(L0_xattn_beta_media), g_lat=cols(L0_xattn_gamma_lat),
        b_lat=cols(L0_xattn_beta_lat), Wq=arr(L0_xattn_Wq), bq=cols(L0_xattn_bq), Wkv=arr(L0_xattn_Wkv),
        bkv=arr(L0_xattn_bkv).reshape(2, -1, P).transpose(2, 0, 1), Wo=arr(L0_xattn_Wo), bo=row(L0_xattn_bo))
    group_b = dict(
        W1T=arr(L0_ffn_W1).T, b1=cols(L0_ffn_b1), W2T=arr(L0_ffn_W2).T, b2=row(L0_ffn_b2), scale=row(L0_ffn_scale),
        WqT=arr(L1_xattn_Wq_w).T, bq1=cols(L1_xattn_Wq_b), WkT=arr(L1_xattn_Wk_w).T, bk1=cols(L1_xattn_Wk_b),
        WvT=arr(L1_xattn_Wv_w).T, bv1=row(L1_xattn_Wv_b), Wg=arr(L1_ffn_Wg), Wu=arr(L1_ffn_Wu), Wd=arr(L1_ffn_Wd),
        Wr=arr(L1_ffn_Wr), temp=row(L1_ffn_temperature))
    tokens = dict(x=arr(x), ctx_in=arr(ctx_1024), ctxT=arr(ctx_1024).transpose(0, 2, 1))

    nc = bacc.Bacc("TRN2", target_bir_lowering=False, num_devices=1)
    arrays, aps = {}, {}
    for name, a in {**tokens, **group_a, **group_b}.items():
        a = np.ascontiguousarray(a)
        arrays["in_" + name] = a
        aps[name] = nc.dram_tensor("in_" + name, a.shape, mybir.dt.from_np(a.dtype), kind="ExternalInput").ap()
    out = nc.dram_tensor("out_x", (B, S, D), F32, kind="ExternalOutput").ap()
    x1 = nc.dram_tensor("x1_between", (B, S, D), F32, kind="Internal").ap()
    lora = nc.dram_tensor("lora_rows", (B, 16, D), F32, kind="Internal").ap()
    program(nc, aps["x"], aps["ctx_in"], aps["ctxT"], [aps[n] for n in group_a], [aps[n] for n in group_b], out, x1,
            lora)
    r = run_bass_kernel_spmd(nc, [arrays], core_ids=[0])
    return r.results[0]["out_x"]
```

```python
import concourse.bass as bass
from concourse import mybir
from contextlib import ExitStack

F32 = mybir.dt.float32
F32R = mybir.dt.float32r
ACT = mybir.ActivationFunctionType
ALU = mybir.AluOpType
AX = mybir.AxisListType

P = 128
B = 16
S = 256
D = 256
ST = S // P
DC = D // P
EPS = 1e-5


def f32(ap):
    return ap.bitcast(F32)


def over(nc, ctx, name, shapes):
    raw = []
    with ExitStack() as first:
        for n, shape in enumerate(shapes):
            raw.append(first.enter_context(nc.sbuf_tensor(f"{name}{n}_raw", shape, F32)))
    return [(r, ctx.enter_context(nc.sbuf_tensor(f"{name}{n}_low", shape, F32R)))
            for n, (r, shape) in enumerate(zip(raw, shapes))]


class Order:

    def __init__(self, names, first, before=None, step=0, turn=None):
        self.names, self.first, self.before = names, first, before
        self.step, self.turn = step, turn

    def at(self, i):
        return self.first + i if self.turn is None else self.first + i + self.turn * self.step

    def bank(self, i, banks):
        return (self.first + i) % banks

    def done(self, name, i):
        if name in self.names[:i]:
            return self.at(len(self.names[:i]) - 1 - self.names[:i][::-1].index(name)) + 1
        back = self.before.index_from_end(name)
        return self.at(-back) + 1

    def index_from_end(self, name):
        return self.names[::-1].index(name) + 1


def latent_attention(nc, x, ctx_in, x1, g_media, b_media, g_lat, b_lat, Wq, bq, Wkv, bkv, Wo, bo, prefetch):
    H = 8
    DH = Wq.shape[1] // H
    INNER = H * DH
    KT = 2 * ST
    SK = KT * P
    QSCALE = float(DH) ** -0.5
    RING = 4
    HALF = INNER // 2

    def slot(h, prev, nxt):
        out = []
        if h + 2 < H or nxt:
            out.append(("K", (h + 2) % H))
        if h % 2 == 0 and (h + 2 < H or nxt):
            out.append(("Q", (h // 2 + 1) % (H // 2)))
        if h > 0 or prev:
            out.append(("O", (h - 1) % H))
        if h < KT:
            out.append(("V", KT + h))
        if h >= H - 2 and nxt:
            out += [("V", 2 * (h - H + 2)), ("V", 2 * (h - H + 2) + 1)]
        return out + [("T", h, 0), ("T", h, 1)]

    def turn_fills(prev, nxt):
        return [f for h in range(H) for f in slot(h, prev, nxt)]

    start = [("K", 0), ("K", 1), ("Q", 0)] + [("V", j) for j in range(KT)]
    sections = {}
    sections["start"] = Order(start, 0)
    sections["first"] = Order(turn_fills(False, True), len(start), sections["start"])
    loop_first = len(start) + len(sections["first"].names)
    loop_names = turn_fills(True, True)
    F = len(loop_names)
    assert F % RING == 0
    TURNS = B - 2
    tail_first = loop_first + F * TURNS

    ctx = ExitStack()
    with ctx:
        def sb(name, shape, dt=F32):
            return ctx.enter_context(nc.sbuf_tensor("a_" + name, shape, dt))

        def pb(name, shape):
            return ctx.enter_context(nc.psum_tensor("a_" + name, shape, F32))

        def sem(name):
            return ctx.enter_context(nc.semaphore("a_" + name))

        (raw_q, wql), (raw_kv, wkvl), (raw_o, wol) = over(
            nc, ctx, "a_weights", ([P, DC, INNER], [P, DC, 2 * INNER], [P, H, D]))
        wqh, wkvh, woh = sb("wqh", [P, DC, INNER], F32R), sb("wkvh", [P, DC, 2 * INNER], F32R), sb("woh", [P, H, D], F32R)
        gm, bm = sb("gm", [P, DC]), sb("bm", [P, DC])
        gl, bl = sb("gl", [P, DC]), sb("bl", [P, DC])
        bq_raw, bq_s = sb("bq_raw", [P, H]), sb("bq_s", [P, H])
        bkv_s = sb("bkv_s", [P, 2, H])
        bo_b = sb("bo_b", [P, D])
        ident = sb("ident", [P, P])
        mhalf = sb("mhalf", [P, ST])
        x_in, c_in = sb("x_in", [P, ST, D]), sb("c_in", [P, ST, D])
        x_ln, x_ln2, c_ln = sb("x_ln", [P, ST, D]), sb("x_ln2", [P, ST, D]), sb("c_ln", [P, ST, D])
        x_res, x_out = sb("x_res", [P, ST, D]), sb("x_out", [P, ST, D])
        stats = sb("stats", [P, 3, ST, 6])
        mv = sb("mv", [P, 3, ST, 2])
        veps, rstd = sb("veps", [P, 3, ST]), sb("rstd", [P, 3, ST])
        aff = sb("aff", [P, 2, DC, S])
        kvh, kvl = sb("kvh", [P, DC, SK], F32R), sb("kvl", [P, DC, SK], F32R)
        kth, ktl = sb("kth", [P, 2, SK], F32R), sb("ktl", [P, 2, SK], F32R)
        qth, qtl = sb("qth", [P, 2, 2, S], F32R), sb("qtl", [P, 2, 2, S], F32R)
        vh, vl = sb("vh", [P, KT, INNER], F32R), sb("vl", [P, KT, INNER], F32R)
        pr = sb("pr", [P, 2, ST, SK])
        pth, ptl = sb("pth", [P, KT, S], F32R), sb("ptl", [P, KT, S], F32R)
        oth, otl = sb("oth", [P, H, S], F32R), sb("otl", [P, H, S], F32R)
        nmax, rsum, rinv = sb("nmax", [P, 2, ST]), sb("rsum", [P, 2, ST]), sb("rinv", [P, 2, ST])

        ring = [pb(f"ring{i}", [P, 512]) for i in range(RING)]
        sim = [pb(f"sim{i}", [P, SK]) for i in range(ST)]
        ps_c = pb("ps_c", [P, DC, S])
        ps_x = pb("ps_x", [P, 512])

        w_in = [sem(f"w_in{i}") for i in range(4)]
        c_small = sem("c_small")
        consts = sem("consts")
        w_hi, w_lo = sem("w_hi"), sem("w_lo")
        ring_full, ring_hi, ring_lo = sem("ring_full"), sem("ring_hi"), sem("ring_lo")
        in_x, in_c, in_res = sem("in_x"), sem("in_c"), sem("in_res")
        dve_step, pool_step, took = sem("dve_step"), sem("pool_step"), sem("took")
        var_ready, rstd_ready = sem("var_ready"), sem("rstd_ready")
        ln_ready, lnT_ready, aff_ready, kv_ready = sem("ln_ready"), sem("lnT_ready"), sem("aff_ready"), sem("kv_ready")
        kv_hi = sem("kv_hi")
        sim_full, max_ready, exp_done, inv_ready, prob_ready = (
            sem(n) for n in ("sim_full", "max_ready", "exp_done", "inv_ready", "prob_ready"))
        wo_full, res_ready, x1_ready, x1_out = sem("wo_full"), sem("res_ready"), sem("x1_ready"), sem("x1_out")

        def sections_of(eng, body):
            body(sections["first"], 0, False, True)
            with eng.Fori(1, B - 1) as b:
                body(Order(loop_names, loop_first - F, sections["first"], F, b), b, True, True)
            loop = Order(loop_names, 0)
            body(Order(turn_fills(True, False), tail_first, loop), B - 1, True, False)

        x_t = x.rearrange("b (t p) d -> b p t d", p=P)
        c_t = ctx_in.rearrange("b (t p) d -> b p t d", p=P)
        x1_t = x1.rearrange("b (t p) d -> b p t d", p=P)

        block = ctx.enter_context(nc.Block())

        @block.sync
        def _(sp):
            sp.sem_inc(x1_out, 16)
            sp.dma_start(c_in[:], c_t[0]).then_inc(in_c, 16)
            sp.dma_start(x_in[:], x_t[0]).then_inc(in_x, 16)
            sp.dma_start(raw_kv[:, :, 0:INNER], Wkv.rearrange("(c p) n -> p c n", p=P)[:, :, 0:INNER])\
                .then_inc(w_in[0], 16)
            for k, (w, n) in enumerate(((g_media, gm), (b_media, bm), (g_lat, gl), (b_lat, bl))):
                sp.dma_start(n[:], w).then_inc(c_small, 16)
            sp.dma_start(bq_raw[:], bq).then_inc(c_small, 16)
            sp.dma_start(bkv_s[:], bkv).then_inc(c_small, 16)
            sp.dma_start(bo_b[:], bo.to_broadcast([P, D])).then_inc(c_small, 16)
            wkv_t = Wkv.rearrange("(c p) n -> p c n", p=P)
            sp.dma_start(raw_q[:], Wq.rearrange("(c p) n -> p c n", p=P)).then_inc(w_in[1], 16)
            sp.dma_start(raw_kv[:, :, INNER:], wkv_t[:, :, INNER:]).then_inc(w_in[2], 16)
            sp.dma_start(raw_o[:], Wo.rearrange("(h p) n -> p h n", p=P)).then_inc(w_in[3], 16)

            def turn(order, b, prev, nxt):
                if nxt:
                    sp.wait_ge(ln_ready, b * 3 + 3)
                    sp.dma_start(c_in[:], c_t[b + 1]).then_inc(in_c, 16)
                    sp.dma_start(x_in[:], x_t[b + 1]).then_inc(in_x, 16)
                if prev:
                    sp.wait_ge(x1_ready, b)
                    sp.dma_start(x1_t[b - 1], x_out[:]).then_inc(x1_out, 16)
                sp.dma_start(x_res[:], x_t[b]).then_inc(in_res, 16)
                if not prev:
                    prefetch(sp)
            sections_of(sp, turn)
            sp.wait_ge(x1_ready, B)
            sp.dma_start(x1_t[B - 1], x_out[:]).then_inc(x1_out, 16)
            sp.wait_ge(x1_out, 16 * B + 16)

        @block.gpsimd
        def _(pool):
            def take(s, value):
                pool.wait_ge(s, value)
                pool.sem_inc(took, 1)

            nc.gpsimd.memset(ident[:], 0.0).then_inc(pool_step, 1)
            nc.gpsimd.memset(mhalf[:], -0.5).then_inc(pool_step, 1)
            pool.wait_ge(pool_step, 2)
            nc.gpsimd.affine_select(out=ident[:], in_=ident[:], compare_op=ALU.not_equal, fill=1.0, base=0,
                                    pattern=[[-1, P]], channel_multiplier=1).then_inc(consts, 1)

            def rstd_of(b, k):
                take(var_ready, b * 3 + k + 1)
                nc.gpsimd.tensor_scalar(veps[:, k, :], mv[:, k, :, 1], EPS, 1.0, ALU.add, ALU.mult)\
                    .then_inc(pool_step, 1)
                pool.wait_ge(pool_step, b * 3 + k + 3)
                nc.gpsimd.tensor_tensor(rstd[:, k, :], veps[:, k, :], mhalf[:], ALU.pow).then_inc(rstd_ready, 1)

            def normalise_probs(b, h):
                for t in range(ST):
                    take(inv_ready, (b * H + h) * ST + t + 1)
                    nc.gpsimd.tensor_scalar(pr[:, h % 2, t, :], pr[:, h % 2, t, :], rinv[:, h % 2, t:t + 1], 1.0,
                                            ALU.mult, ALU.mult).then_inc(prob_ready, 1)

            for k in range(3):
                rstd_of(0, k)
            normalise_probs(0, 0)
            pool.wait_ge(c_small, 16 * 7)

            def turn(order, b, prev, nxt):
                for h in range(H):
                    if nxt and h < 3:
                        rstd_of(b + 1, h)
                    if h + 1 < H:
                        normalise_probs(b, h + 1)
                    elif nxt:
                        normalise_probs(b + 1, 0)
                    if h == 3:
                        pool.wait_ge(in_res, b * 16 + 16)
                        if prev:
                            pool.wait_ge(x1_ready, b)
                        nc.gpsimd.tensor_tensor(x_res[:], x_res[:], bo_b[:].unsqueeze(1).to_broadcast([P, ST, D]),
                                                ALU.add).then_inc(res_ready, 1)
            sections_of(pool, turn)

        @block.scalar
        def _(act):
            act.wait_ge(c_small, 16 * 7)

            def affine(b, k):
                g, bb = ((gm, bm), (gl, bl))[k]
                act.wait_ge(lnT_ready, b * 2 + k + 1)
                for c in range(DC):
                    src = ps_c[:, c, :] if k == 0 else ps_x[:, c * S:(c + 1) * S]
                    last = nc.scalar.activation(aff[:, k, c, :], src, ACT.Identity, bias=bb[:, c:c + 1],
                                                scale=g[:, c:c + 1])
                last.then_inc(aff_ready, 1)

            act.wait_ge(w_in[0], 16)
            nc.scalar.activation(wkvh[:, :, 0:INNER], raw_kv[:, :, 0:INNER], ACT.Copy).then_inc(w_hi, 1)
            affine(0, 0)
            affine(0, 1)
            nc.scalar.activation(bq_s[:], bq_raw[:], ACT.Copy, scale=QSCALE).then_inc(w_hi, 1)
            act.wait_ge(w_in[1], 16)
            nc.scalar.activation(wqh[:], raw_q[:], ACT.Copy, scale=QSCALE).then_inc(w_hi, 1)
            act.wait_ge(w_in[2], 16)
            nc.scalar.activation(wkvh[:, :, INNER:], raw_kv[:, :, INNER:], ACT.Copy).then_inc(w_hi, 1)
            act.wait_ge(w_in[3], 16)
            nc.scalar.activation(woh[:], raw_o[:], ACT.Copy).then_inc(w_hi, 1)
            act.wait_ge(w_hi, 5)

            def high_half(order, i):
                name = order.names[i]
                bank = ring[order.bank(i, RING)]
                act.wait_ge(ring_full, order.at(i) + 1)
                h = name[1]
                if name[0] == "K":
                    nc.scalar.activation(kth[:, h % 2], bank[:], ACT.Identity, bias=bkv_s[:, 0, h:h + 1])\
                        .then_inc(ring_hi, 1)
                elif name[0] == "Q":
                    for j in range(2):
                        last = nc.scalar.activation(qth[:, h % 2, j], bank[:, j * S:(j + 1) * S], ACT.Identity,
                                                    bias=bq_s[:, 2 * h + j:2 * h + j + 1])
                    last.then_inc(ring_hi, 1)
                elif name[0] == "V":
                    nc.scalar.activation(vh[:, h % KT, h // KT * HALF:(h // KT + 1) * HALF], bank[:], ACT.Copy)\
                        .then_inc(ring_hi, 1)
                elif name[0] == "T":
                    nc.scalar.activation(pth[:, :, name[2] * P:(name[2] + 1) * P],
                                         bank[:].rearrange("p (k q) -> p k q", k=KT), ACT.Copy).then_inc(ring_hi, 1)
                else:
                    nc.scalar.activation(oth[:, h], bank[:, 0:S], ACT.Identity, bias=bkv_s[:, 1, h:h + 1])\
                        .then_inc(ring_hi, 1)

            def exps(b, h):
                for t in range(ST):
                    act.wait_ge(max_ready, (b * H + h) * ST + t + 1)
                    nc.scalar.activation(pr[:, h % 2, t, :], sim[t][:], ACT.Exp, bias=nmax[:, h % 2, t:t + 1],
                                         accum_out=rsum[:, h % 2, t:t + 1]).then_inc(exp_done, 1)

            for i in range(len(start)):
                high_half(sections["start"], i)
            exps(0, 0)

            def turn(order, b, prev, nxt):
                i = 0
                for h in range(H):
                    if h + 1 < H:
                        exps(b, h + 1)
                    elif nxt:
                        exps(b + 1, 0)
                    n = len(slot(h, prev, nxt))
                    for j in range(n):
                        high_half(order, i + j)
                        if j == n - 1 and h == H - 4 and nxt:
                            affine(b + 1, 0)
                            affine(b + 1, 1)
                    i += n
            sections_of(act, turn)
            high_half(Order([("O", H - 1)], tail_first + len(turn_fills(True, False))), 0)

        @block.vector
        def _(dve):
            def take(s, value):
                dve.wait_ge(s, value)
                dve.sem_inc(took, 1)

            def norm_stats(b, k):
                src = (c_in, x_in, x_ln)[k]
                if k == 2:
                    dve.wait_ge(ln_ready, b * 3 + 2)
                else:
                    dve.wait_ge((in_c, in_x)[k], b * 16 + 16)
                for t in range(ST):
                    last = nc.vector.bn_stats(stats[:, k, t, :], src[:, t, :])
                last.then_inc(dve_step, 1)
                take(dve_step, b * 3 + k + 1)
                for t in range(ST):
                    last = nc.vector.bn_aggr(mv[:, k, t, :], stats[:, k, t, :])
                last.then_inc(var_ready, 1)

            def norm_apply(b, k):
                src, dst = ((c_in, c_ln), (x_in, x_ln), (x_ln, x_ln2))[k]
                dve.wait_ge(rstd_ready, b * 3 + k + 1)
                for t in range(ST):
                    last = nc.vector.tensor_scalar(dst[:, t, :], src[:, t, :], mv[:, k, t, 0:1],
                                                   rstd[:, k, t:t + 1], ALU.subtract, ALU.mult)
                last.then_inc(ln_ready, 1)

            def kv_halves(b, k):
                dve.wait_ge(aff_ready, b * 2 + k + 1)
                nc.vector.tensor_copy(kvh[:, :, k * S:(k + 1) * S], aff[:, k]).then_inc(kv_hi, 1)
                dve.wait_ge(kv_hi, b * 2 + k + 1)
                nc.vector.tensor_tensor(kvl[:, :, k * S:(k + 1) * S], aff[:, k], f32(kvh[:, :, k * S:(k + 1) * S]),
                                        ALU.subtract).then_inc(kv_ready, 1)

            norm_stats(0, 0)
            norm_stats(0, 1)
            norm_apply(0, 0)
            norm_apply(0, 1)
            norm_stats(0, 2)
            norm_apply(0, 2)
            dve.wait_ge(w_hi, 1)
            nc.vector.tensor_tensor(wkvl[:, :, 0:INNER], raw_kv[:, :, 0:INNER], f32(wkvh[:, :, 0:INNER]),
                                    ALU.subtract).then_inc(w_lo, 1)
            kv_halves(0, 0)
            kv_halves(0, 1)
            dve.wait_ge(w_hi, 3)
            nc.vector.scalar_tensor_tensor(wql[:].rearrange("p c n -> p (c n)"),
                                           raw_q[:].rearrange("p c n -> p (c n)"), QSCALE,
                                           f32(wqh[:]).rearrange("p c n -> p (c n)"), ALU.mult, ALU.subtract)\
                .then_inc(w_lo, 1)
            dve.wait_ge(w_hi, 4)
            nc.vector.tensor_tensor(wkvl[:, :, INNER:], raw_kv[:, :, INNER:], f32(wkvh[:, :, INNER:]),
                                    ALU.subtract).then_inc(w_lo, 1)
            dve.wait_ge(w_hi, 5)
            nc.vector.tensor_tensor(wol[:], raw_o[:], f32(woh[:]), ALU.subtract).then_inc(w_lo, 1)

            def low_half(order, i):
                name = order.names[i]
                bank = ring[order.bank(i, RING)]
                dve.wait_ge(ring_hi, order.at(i) + 1)
                h = name[1]
                if name[0] == "K":
                    nc.vector.scalar_tensor_tensor(ktl[:, h % 2], bank[:], bkv_s[:, 0, h:h + 1], f32(kth[:, h % 2]),
                                                   ALU.add, ALU.subtract).then_inc(ring_lo, 1)
                elif name[0] == "Q":
                    for j in range(2):
                        last = nc.vector.scalar_tensor_tensor(qtl[:, h % 2, j], bank[:, j * S:(j + 1) * S],
                                                              bq_s[:, 2 * h + j:2 * h + j + 1],
                                                              f32(qth[:, h % 2, j]), ALU.add, ALU.subtract)
                    last.then_inc(ring_lo, 1)
                elif name[0] == "V":
                    cols = slice(h // KT * HALF, (h // KT + 1) * HALF)
                    nc.vector.tensor_tensor(vl[:, h % KT, cols], bank[:], f32(vh[:, h % KT, cols]),
                                            ALU.subtract).then_inc(ring_lo, 1)
                elif name[0] == "T":
                    cols = slice(name[2] * P, (name[2] + 1) * P)
                    nc.vector.tensor_tensor(ptl[:, :, cols], bank[:].rearrange("p (k q) -> p k q", k=KT),
                                            f32(pth[:, :, cols]), ALU.subtract).then_inc(ring_lo, 1)
                else:
                    nc.vector.scalar_tensor_tensor(otl[:, h], bank[:, 0:S], bkv_s[:, 1, h:h + 1], f32(oth[:, h]),
                                                   ALU.add, ALU.subtract).then_inc(ring_lo, 1)

            def maxima(b, h):
                for t in range(ST):
                    dve.wait_ge(sim_full, (b * H + h) * ST + t + 1)
                    nc.vector.tensor_reduce(nmax[:, h % 2, t:t + 1], sim[t][:], AX.X, ALU.max, negate=True)\
                        .then_inc(max_ready, 1)

            def inverses(b, h, early):
                for t in range(ST):
                    n = (b * H + h) * ST + t + 1
                    dve.wait_ge(exp_done, n)
                    if not early:
                        dve.wait_ge(prob_ready, n - 2 * ST)
                    nc.vector.reciprocal(rinv[:, h % 2, t:t + 1], rsum[:, h % 2, t:t + 1]).then_inc(inv_ready, 1)

            def residual(b):
                dve.wait_ge(wo_full, b + 1)
                dve.wait_ge(res_ready, b + 1)
                dve.wait_ge(x1_out, b * 16 + 16)
                nc.vector.tensor_tensor(x_out[:].rearrange("p t d -> p (t d)"), ps_x[:],
                                        x_res[:].rearrange("p t d -> p (t d)"), ALU.add).then_inc(x1_ready, 1)

            for i in range(len(start)):
                low_half(sections["start"], i)
            maxima(0, 0)
            inverses(0, 0, True)

            def turn(order, b, prev, nxt):
                i = 0
                for h in range(H):
                    if h + 1 < H:
                        maxima(b, h + 1)
                    elif nxt:
                        maxima(b + 1, 0)
                    if nxt:
                        if 1 <= h <= 3:
                            norm_apply(b + 1, h - 1)
                        if h < 3:
                            norm_stats(b + 1, h)
                    if h == H - 3 and nxt:
                        dve.wait_ge(ring_full, order.at(i) + 1)
                        kv_halves(b + 1, 0)
                    n = len(slot(h, prev, nxt))
                    for j in range(n):
                        low_half(order, i + j)
                        if j == 0:
                            if h + 1 < H:
                                inverses(b, h + 1, not prev and h == 0)
                            elif nxt:
                                inverses(b + 1, 0, False)
                        if j == 0 and h == H - 3 and nxt:
                            kv_halves(b + 1, 1)
                        if j == 1 and h == 1 and prev:
                            residual(b - 1)
                    i += n
            sections_of(dve, turn)
            low_half(Order([("O", H - 1)], tail_first + len(turn_fills(True, False))), 0)
            residual(B - 1)

        @block.tensor
        def _(pe):
            def product(out, parts, left_h, left_l, right_h, right_l):
                for n, part in enumerate(parts):
                    lh, ll, rh, rl = left_h(part), left_l(part), right_h(part), right_l(part)
                    nc.tensor.matmul(out, lh, rh, start=(n == 0), stop=False)
                    nc.tensor.matmul(out, lh, rl, start=False, stop=False)
                    last = nc.tensor.matmul(out, ll, rh, start=False, stop=(n == len(parts) - 1))
                return last

            def transposes(b):
                for k, (ln, ps) in enumerate(((c_ln, 0), (x_ln2, 1))):
                    pe.wait_ge(ln_ready, b * 3 + (1 if k == 0 else 3))
                    for c in range(DC):
                        for t in range(ST):
                            out = ps_c[:, c, t * P:(t + 1) * P] if k == 0 else \
                                ps_x[:, c * S + t * P:c * S + (t + 1) * P]
                            last = nc.tensor.transpose(out, ln[:, t, c * P:(c + 1) * P], ident[:])
                    last.then_inc(lnT_ready, 1)

            def scores(b, h, order, i):
                pe.wait_ge(ring_lo, order.done(("K", h), i))
                pe.wait_ge(ring_lo, order.done(("Q", h // 2), i))
                for t in range(ST):
                    if not (isinstance(b, int) and b == 0 and h == 0):
                        pe.wait_ge(exp_done, (b * H + h) * ST + t + 1 - ST)
                    q = slice(t * P, (t + 1) * P)
                    product(sim[t][:], [0], lambda _: qth[:, h // 2 % 2, h % 2, q], lambda _: qtl[:, h // 2 % 2, h % 2, q],
                            lambda _: kth[:, h % 2], lambda _: ktl[:, h % 2]).then_inc(sim_full, 1)

            def fill(order, i, b):
                name = order.names[i]
                bank = ring[order.bank(i, RING)]
                h = name[1]
                if order.turn is not None or order.first + i >= RING:
                    pe.wait_ge(ring_lo, order.at(i) + 1 - RING)
                if name[0] == "K":
                    cols = slice(h * DH, (h + 1) * DH)
                    last = product(bank[:], range(DC), lambda c: wkvh[:, c, cols], lambda c: wkvl[:, c, cols],
                                   lambda c: kvh[:, c, :], lambda c: kvl[:, c, :])
                elif name[0] == "Q":
                    for j in range(2):
                        cols = slice((2 * h + j) * DH, (2 * h + j + 1) * DH)
                        last = product(bank[:, j * S:(j + 1) * S], range(DC), lambda c: wqh[:, c, cols],
                                       lambda c: wql[:, c, cols], lambda c: kvh[:, c, S:], lambda c: kvl[:, c, S:])
                elif name[0] == "V":
                    rows = slice(h % KT * P, (h % KT + 1) * P)
                    cols = slice(INNER + h // KT * HALF, INNER + (h // KT + 1) * HALF)
                    last = product(bank[:], range(DC), lambda c: kvh[:, c, rows], lambda c: kvl[:, c, rows],
                                   lambda c: wkvh[:, c, cols], lambda c: wkvl[:, c, cols])
                elif name[0] == "T":
                    t = name[2]
                    pe.wait_ge(prob_ready, (b * H + h) * ST + t + 1)
                    for k in range(KT):
                        last = nc.tensor.transpose(bank[:, k * P:(k + 1) * P], pr[:, h % 2, t, k * P:(k + 1) * P],
                                                   ident[:])
                else:
                    pe.wait_ge(ring_lo, order.done(("T", h, ST - 1), i))
                    cols = slice(h * DH, (h + 1) * DH)
                    last = product(bank[:, 0:S], range(KT), lambda k: vh[:, k, cols], lambda k: vl[:, k, cols],
                                   lambda k: pth[:, k, :], lambda k: ptl[:, k, :])
                last.then_inc(ring_full, 1)

            def project_out(b, order, i):
                pe.wait_ge(ring_lo, order.done(("O", H - 1), i))
                for t in range(ST):
                    q = slice(t * P, (t + 1) * P)
                    last = product(ps_x[:, t * D:(t + 1) * D], range(H), lambda h: oth[:, h, q],
                                   lambda h: otl[:, h, q], lambda h: woh[:, h], lambda h: wol[:, h])
                last.then_inc(wo_full, 1)

            pe.wait_ge(consts, 1)
            transposes(0)
            pe.wait_ge(kv_ready, 2)
            for i in range(len(start)):
                pe.wait_ge(w_lo, {"K": 1, "Q": 2, "V": 3}[start[i][0]])
                fill(sections["start"], i, 0)
                if start[i] == ("V", 0):
                    scores(0, 0, sections["start"], i)
            pe.wait_ge(w_lo, 4)

            def turn(order, b, prev, nxt):
                i = 0
                for h in range(H):
                    if h + 1 < H:
                        scores(b, h + 1, order, i)
                    elif nxt:
                        scores(b + 1, 0, order, i)
                    n = len(slot(h, prev, nxt))
                    for j in range(n):
                        if nxt and h == H - 2 and j == 0:
                            pe.wait_ge(kv_ready, b * 2 + 4)
                        if h == 1 and j == 1 and prev:
                            project_out(b - 1, order, i + j)
                        fill(order, i + j, b)
                        if j == 0 and h == H - 4 and nxt:
                            if prev:
                                pe.wait_ge(x1_ready, b)
                            transposes(b + 1)
                    i += n
            sections_of(pe, turn)
            end = Order([("O", H - 1)], tail_first + len(turn_fills(True, False)),
                        Order(turn_fills(True, False), 0))
            fill(end, 0, B - 1)
            project_out(B - 1, end, 1)


class ExpertWeights:
    EARLY = 4

    def __init__(self, nc, ctx, W1T, b1, W2T, b2, scale, WqT, bq, WkT, bk, WvT, bv, Wg, Wu, Wd, Wr, temp):
        self.sets = [(WqT, WkT, WvT)] + [(Wg[e], Wu[e], Wd[e]) for e in range(Wg.shape[0])]
        self.raw, self.low = zip(*over(nc, ctx, "weights", [[P, 3, DC, D]] * (self.EARLY + 1)))
        self.loaded = [ctx.enter_context(nc.semaphore(f"weights_in{n}")) for n in range(len(self.sets))]

    def add_late(self, nc, ctx):
        raw, low = zip(*over(nc, ctx, "weights_late", [[P, 3, DC, D]] * (len(self.sets) - self.EARLY - 1)))
        self.raw, self.low = self.raw + raw, self.low + low

    def load(self, eng, n):
        for j, w in enumerate(self.sets[n]):
            eng.dma_start(self.raw[n][:, j], w.rearrange("(c p) d -> p c d", p=P)).then_inc(self.loaded[n], 16)

    def prefetch(self, eng):
        for n in range(self.EARLY + 1):
            self.load(eng, n)


def ffn_attention_experts(nc, x1, ctxT, out, lora, W1T, b1, W2T, b2, scale, WqT, bq, WkT, bk, WvT, bv, Wg, Wu, Wd, Wr,
                          temp, weights):
    HID = W1T.shape[1]
    HC = HID // P
    E = Wg.shape[0]
    NL = 4
    A4 = D // NL
    GOLDEN_CENTER = 1.0 / 2.718281828459045
    GOLDEN_LOWER = 0.5 - 0.2876820724517809
    GOLDEN_UPPER = 0.5
    QSCALE = float(D) ** -0.5
    RING = 5
    STAGES = 3

    def slot(e, nb, nn):
        if e == 0 and nb:
            return [("H", n) for n in range(HC // 2)], []
        if e == 1 and nb:
            return [], [("Y",)]
        if e == 2 and nb:
            return [("K",), ("V",)], [("B",)]
        if e == 3 and nb:
            return [("Q",)], [("S",)]
        if e == 4 and nb:
            return [("T",)] + ([("A",)] if nn else []), [("O",)]
        if e == 5 and nb:
            return [], [("C",)]
        if e == 6 and nb:
            return [], [("R",)]
        return [], []

    def turn_fills(nb, nn):
        return [f for e in range(E) for part in slot(e, nb, nn) for f in part]

    ONLY_DVE = ("Y", "O")

    class Fills(Order):
        def __init__(self, names, first, hi_first, before, step=0, hi_step=0, turn=None):
            super().__init__(names, first, before, step, turn)
            self.hi_first, self.hi_step = hi_first, hi_step

        def hi_at(self, i):
            n = self.hi_first + sum(f[0] not in ONLY_DVE for f in self.names[:i])
            return n if self.turn is None else n + self.turn * self.hi_step

    names_all = turn_fills(True, True)
    F = len(names_all)
    FH = sum(f[0] not in ONLY_DVE for f in names_all)
    assert F % RING == 0
    start = Fills([("A",)], 0, 0, None)

    ctx = ExitStack()
    with ctx:
        def sb(name, shape, dt=F32):
            return ctx.enter_context(nc.sbuf_tensor("b_" + name, shape, dt))

        def pb(name, shape):
            return ctx.enter_context(nc.psum_tensor("b_" + name, shape, F32))

        def sem(name):
            return ctx.enter_context(nc.semaphore("b_" + name))

        w1h, w1l = sb("w1h", [P, DC, HID], F32R), sb("w1l", [P, DC, HID], F32R)
        w2h, w2l = sb("w2h", [P, HC, D], F32R), sb("w2l", [P, HC, D], F32R)
        weights.add_late(nc, ctx)
        wqkvh, wqkvl = sb("wqkvh", [P, 3, DC, D], F32R), weights.low[0]
        weh, wel = sb("weh", [P, E, 3, DC, D], F32R), weights.low[1:]
        wrh, wrl = sb("wrh", [P, DC, E], F32R), sb("wrl", [P, DC, E], F32R)
        stage = sb("stage", [P, STAGES, 2 * D])
        even = [sb(f"even{j}", [P, NL, D]) for j in range(2)]
        b1_s, bq_s, bk_s = sb("b1_s", [P, HC]), sb("bq_s", [P, DC]), sb("bk_s", [P, DC])
        b2_b, bv_b = sb("b2_b", [P, D]), sb("bv_b", [P, D])
        lscale, tinv, thalf = sb("lscale", [P, 1]), sb("tinv", [P, 1]), sb("thalf", [P, 1])
        ident = sb("ident", [P, P])
        mhalf = sb("mhalf", [P, ST])
        index = sb("index", [P, E])
        x1_s, x2_s, acc = sb("x1_s", [P, ST, D]), sb("x2_s", [P, ST, D]), sb("acc", [P, ST, D])
        ln = sb("ln", [P, ST, D])
        stats, mv = sb("stats", [P, ST, 6]), sb("mv", [P, ST, 2])
        xth, xtl = sb("xth", [P, DC, S], F32R), sb("xtl", [P, DC, S], F32R)
        xch, xcl = sb("xch", [P, DC, S], F32R), sb("xcl", [P, DC, S], F32R)
        odd = sb("odd", [P, DC, 2 * NL])
        hh, hl = sb("hh", [P, HC, S], F32R), sb("hl", [P, HC, S], F32R)
        ct_raw = sb("ct_raw", [P, DC, S])
        cth, ctl = xth, xtl
        pr = sb("pr", [P, ST, S])
        gel = [sb("gel", [P, ST * S])[:], pr[:].rearrange("p t s -> p (t s)")]
        rows = sb("rows", [P, 9, ST])
        veps, rstd, nmax, rsum, rinv, wsum, fsum, none_in, some_in = (rows[:, n, :] for n in range(9))
        act_e = sb("act_e", [P, 2, 2 * S])
        heh, hel = sb("heh", [P, 2, 2, S], F32R), sb("hel", [P, 2, 2, S], F32R)
        sig, dist, near, wz, fb = (sb(n, [P, ST, E]) for n in ("sig", "dist", "near", "wz", "fb"))
        top, mask, wts = (sb(n, [P, ST, E]) for n in ("top", "mask", "wts"))
        top_at = sb("top_at", [P, ST, E], mybir.dt.uint32)
        top_f = sb("top_f", [P, ST, 2])
        wr_raw, bq_raw = mask, none_in
        Q, K, V, PT = 0, 2, 4, 6

        ring = [pb(f"ring{i}", [P, 512]) for i in range(RING)]
        ps_g, ps_u, ps_d = pb("ps_g", [P, 512]), pb("ps_u", [P, 512]), pb("ps_d", [P, 512])

        small_in = sem("small_in")
        stage_in = [sem(f"stage_in{j}") for j in range(STAGES)]
        warm_hi, warm_lo = sem("warm_hi"), sem("warm_lo")
        stage_hi, stage_lo, stage_sum = sem("stage_hi"), sem("stage_lo"), sem("stage_sum")
        even_in = [sem(f"even_in{j}") for j in range(2)]
        lora_out = sem("lora_out")
        consts, w_ready = sem("consts"), sem("w_ready")
        ring_full, ring_hi, ring_lo = sem("ring_full"), sem("ring_hi"), sem("ring_lo")
        x1_in, x1_biased, x2_ready, x2_biased, x3_ready = (
            sem(n) for n in ("x1_in", "x1_biased", "x2_ready", "x2_biased", "x3_ready"))
        ct_in, ct_hi, ct_lo = sem("ct_in"), sem("ct_hi"), sem("ct_lo")
        stats_ready, var_ready, rstd_ready, ln_ready = (
            sem(n) for n in ("stats_ready", "var_ready", "rstd_ready", "ln_ready"))
        odd_ready = sem("odd_ready")
        gel_ready, max_ready = sem("gel_ready"), sem("max_ready")
        gate_full, up_full, silu_done, he_ready, he_hi, he_lo, down_full, acc_ready = (
            sem(n) for n in ("gate_full", "up_full", "silu_done", "he_ready", "he_hi", "he_lo", "down_full", "acc_ready"))
        dist_ready, exps_ready, wts_ready = sem("dist_ready"), sem("exps_ready"), sem("wts_ready")
        route_step = sem("route_step")
        pool_step, took = sem("pool_step"), sem("took")
        out_done = sem("out_done")

        def sections_of(eng, body):
            first = Fills(names_all, 1, 1, start)
            body(first, 0, False, True, True)
            with eng.Fori(1, B - 1) as t:
                body(Fills(names_all, 1, 1, first, F, FH, t), t, True, True, True)
            loop = Fills(names_all, 0, 0, None)
            last = Fills(turn_fills(True, False), 1 + F * (B - 1), 1 + FH * (B - 1), loop)
            body(last, B - 1, True, True, False)
            body(Fills([], 0, 0, last), B, True, False, False)

        def ln_no(t, which):
            if isinstance(t, int) and t == B - 1:
                return 1 + 3 * t + {"B": 0, "C": 1}[which]
            return 1 + t * 3 + {"B": 0, "A": 1, "C": 2}[which]

        CHUNKS = 2 * NL
        PIECES = {(5, 1): (0,), (6, 1): (1,), (6, 2): (2,), (7, 1): (3,)}
        LATE = {(0, 0): (4,), (0, 1): (5,), (0, 2): (6,), (1, 0): (7,)}
        LATE_FIRST = {(0, 0): (4,), (0, 1): (5,), (0, 2): (6, 7)}
        SUMS = {(5, 0): (0,), (5, 1): (1,)}
        DVE_SUMS = 2
        EARLY_PIECES, LATE_PIECES = range(7), range(7, CHUNKS)
        WARM_SLOTS = (10, 8, 0, 6)

        def warm_weight(k):
            n = k // 3 - 1
            parts = (weights.raw[0], wqkvh, wqkvl) if k < 3 else (weights.raw[n + 1], weh[:, n], wel[n])
            return [w[:, k % 3].rearrange("p c d -> p (c d)") for w in parts]

        def warm_pieces(e):
            first = 3 + sum(WARM_SLOTS[:e])
            return range(first, first + sum(WARM_SLOTS[e:e + 1]))

        WARM = 3 * (E + 1)

        def piece_in(n, k):
            return (n * len(range(k % STAGES, CHUNKS, STAGES)) + k // STAGES + 1) * 16

        x1_t = x1.rearrange("b (t p) d -> b p t d", p=P)
        out_t = out.rearrange("b (t p) d -> b p t d", p=P)
        ct_t = ctxT.rearrange("b (c p) s -> b p c s", p=P)

        block = ctx.enter_context(nc.Block())

        @block.sync
        def _(sp):
            def take(s, value):
                sp.wait_ge(s, value)
                sp.sem_inc(took, 1)

            def weights_of(n, first, pieces):
                for k in pieces:
                    if k >= STAGES or not first:
                        take(stage_lo, n * CHUNKS + max(k - STAGES + 1, 0))
                    if k < NL:
                        src = W1T[k // 2 * P:(k // 2 + 1) * P, k % 2 * 2 * D:(k % 2 + 1) * 2 * D]
                        dst = stage[:, k % STAGES, :]
                    else:
                        g = k - NL
                        src = W2T[g * 2 * P:(g + 1) * 2 * P, :].rearrange("(c p) d -> p c d", p=P)
                        dst = stage[:, k % STAGES, :].rearrange("p (c d) -> p c d", c=2)
                    sp.dma_start(dst, src).then_inc(stage_in[k % STAGES], 16)
                    if k == 1:
                        take(lora_out, n * 16 + 16)
                        for j in range(2):
                            sp.dma_start(even[j][:], lora[n, 2 * NL * j:2 * NL * (j + 1):2, :].unsqueeze(0)
                                         .to_broadcast([P, NL, D])).then_inc(even_in[j], 16)

            sp.sem_inc(out_done, 16)
            sp.dma_start(x1_s[:], x1_t[0]).then_inc(x1_in, 16)
            sp.dma_start(ct_raw[:], ct_t[0]).then_inc(ct_in, 16)
            for dst, src in ((b1_s, b1), (bq_raw, bq), (bk_s, bk)):
                sp.dma_start(dst[:], src).then_inc(small_in, 16)
            for dst, src in ((b2_b, b2), (bv_b, bv)):
                sp.dma_start(dst[:], src.to_broadcast([P, D])).then_inc(small_in, 16)
            sp.dma_start(lscale[:], scale.to_broadcast([P, 1])).then_inc(small_in, 16)
            sp.dma_start(tinv[:], temp.to_broadcast([P, 1])).then_inc(small_in, 16)
            sp.dma_start(wr_raw[:], Wr.rearrange("(c p) e -> p c e", p=P)).then_inc(small_in, 16)
            sp.wait_ge(ln_ready, 1)
            sp.dma_start(lora[0], ln[1:1 + 4 * NL, 0, :]).then_inc(lora_out, 16)
            weights_of(0, True, range(CHUNKS))

            def turn(fills, t, experts, nb, nn):
                if experts and nb:
                    weights_of(t, False, LATE_PIECES)
                if nn:
                    take(ct_lo, t + 1)
                    sp.dma_start(ct_raw[:], ct_t[t + 1]).then_inc(ct_in, 16)
                    take(x2_ready, t + 1)
                    sp.dma_start(x1_s[:], x1_t[t + 1]).then_inc(x1_in, 16)
                    take(ln_ready, ln_no(t, "A") + 1)
                    sp.dma_start(lora[t + 1], ln[1:1 + 4 * NL, 0, :]).then_inc(lora_out, 16)
                    weights_of(t + 1, False, EARLY_PIECES)
                if experts:
                    take(acc_ready, t * E + 1)
                    sp.dma_start(out_t[t - 1], acc[:]).then_inc(out_done, 16)
            sections_of(sp, turn)
            sp.wait_ge(out_done, 16 * B + 16)

        @block.gpsimd
        def _(pool):
            def take(s, value):
                pool.wait_ge(s, value)
                pool.sem_inc(took, 1)

            nc.gpsimd.memset(ident[:], 0.0).then_inc(pool_step, 1)
            nc.gpsimd.memset(mhalf[:], -0.5).then_inc(pool_step, 1)
            pool.wait_ge(pool_step, 2)
            nc.gpsimd.affine_select(out=ident[:], in_=ident[:], compare_op=ALU.not_equal, fill=1.0, base=0,
                                    pattern=[[-1, P]], channel_multiplier=1).then_inc(consts, 1)
            for e in range(E):
                last = nc.gpsimd.memset(index[:, e:e + 1], float(e))
            last.then_inc(consts, 1)
            pool.wait_ge(consts, 2)

            def rstd_of(n, base):
                take(var_ready, n + 1)
                nc.gpsimd.tensor_scalar(veps[:], mv[:, :, 1], EPS, 1.0, ALU.add, ALU.mult).then_inc(pool_step, 1)
                pool.wait_ge(pool_step, base + 1)
                nc.gpsimd.tensor_tensor(rstd[:], veps[:], mhalf[:], ALU.pow).then_inc(rstd_ready, 1)

            def bias_x1(n, l):
                pool.wait_ge(ln_ready, l + 1)
                nc.gpsimd.tensor_tensor(x1_s[:], x1_s[:], b2_b[:].unsqueeze(1).to_broadcast([P, ST, D]), ALU.add)\
                    .then_inc(x1_biased, 1)

            def low_rank(n, base, pieces):
                for k in pieces:
                    if k in (DVE_SUMS, NL):
                        take(odd_ready, n + 1)
                        take(even_in[k // NL], n * 16 + 16)
                    if k < NL:
                        for j in range(2):
                            i = k % 2 * 2 + j
                            last = nc.gpsimd.tensor_scalar(ln[:, j, :], even[0][:, i, :], odd[:, k // 2, i:i + 1], 1.0,
                                                           ALU.mult, ALU.mult)
                    else:
                        for c in range(DC):
                            last = nc.gpsimd.tensor_tensor(
                                ln[:, c, :].rearrange("p (i a) -> p i a", i=NL),
                                even[1][:].rearrange("p i (a m) -> p i a m", m=4)[:, :, :, k - NL],
                                odd[:, c, NL:].unsqueeze(2).to_broadcast([P, NL, A4]), ALU.mult)
                    last.then_inc(pool_step, 1)
                    pool.wait_ge(pool_step, base + k - DVE_SUMS + 1)
                    pool.wait_ge(stage_in[k % STAGES], piece_in(n, k))
                    if k == DVE_SUMS:
                        take(stage_sum, n * CHUNKS + k)
                    nc.gpsimd.tensor_tensor(stage[:, k % STAGES, :], stage[:, k % STAGES, :],
                                            ln[:].rearrange("p c d -> p (c d)"), ALU.add).then_inc(stage_sum, 1)
                    take(stage_sum, n * CHUNKS + k + 1)

            rstd_of(0, 2)
            pool.wait_ge(small_in, 16 * 8)
            bias_x1(0, 0)
            pool.wait_ge(ring_full, 1)
            pool.wait_ge(lora_out, 16)
            low_rank(0, 3, range(DVE_SUMS, CHUNKS))
            SUMMED = CHUNKS - DVE_SUMS
            START = 3 + SUMMED
            OWN_TURN = 2

            def turn(fills, t, experts, nb, nn):
                base = START + t * (3 + SUMMED) - (OWN_TURN if experts else 0)
                if nb and experts:
                    low_rank(t, base - (SUMMED - OWN_TURN), range(CHUNKS - OWN_TURN, CHUNKS))
                    base = base + OWN_TURN
                if nb:
                    rstd_of(ln_no(t, "B"), base)
                    pool.wait_ge(ln_ready, ln_no(t, "B") + 1)
                    nc.gpsimd.tensor_tensor(x2_s[:], x2_s[:], bv_b[:].unsqueeze(1).to_broadcast([P, ST, D]),
                                            ALU.add).then_inc(x2_biased, 1)
                if nn:
                    rstd_of(ln_no(t, "A"), base + 1)
                    bias_x1(t + 1, ln_no(t, "A"))
                if nb:
                    rstd_of(ln_no(t, "C"), base + (2 if nn else 1))
                if nn:
                    pool.wait_ge(ring_full, fills.done(("C",), len(fills.names)))
                    low_rank(t + 1, base + 3, range(DVE_SUMS, CHUNKS - OWN_TURN))
            sections_of(pool, turn)

        @block.scalar
        def _(act):
            def warm_high(k):
                act.wait_ge(weights.loaded[k // 3], 3 * 16)
                raw, dh, _ = warm_weight(k)
                nc.scalar.activation(dh, raw, ACT.Copy, scale=QSCALE if k == 0 else 1.0).then_inc(warm_hi, 1)

            act.wait_ge(small_in, 16 * 8)
            nc.scalar.activation(bq_s[:], bq_raw[:], ACT.Copy, scale=QSCALE).then_inc(stage_hi, 1)
            nc.scalar.activation(wrh[:], wr_raw[:], ACT.Copy).then_inc(stage_hi, 1)

            def weights_high(n, k):
                act.wait_ge(stage_sum, n * CHUNKS + k + 1)
                if k < NL:
                    dst = w1h[:, k // 2, k % 2 * 2 * D:(k % 2 + 1) * 2 * D]
                else:
                    dst = w2h[:, 2 * (k - NL):2 * (k - NL) + 2, :].rearrange("p c d -> p (c d)")
                nc.scalar.activation(dst, stage[:, k % STAGES, :], ACT.Copy).then_inc(stage_hi, 1)

            def context_high(t):
                act.wait_ge(ct_in, t * 16 + 16)
                nc.scalar.activation(cth[:], ct_raw[:], ACT.Copy).then_inc(ct_hi, 1)

            def silu(i, e):
                act.wait_ge(gate_full, i * E + e + 1)
                nc.scalar.activation(act_e[:, e % 2, :], ps_g[:], ACT.Silu).then_inc(silu_done, 1)

            def hidden_high(i, e):
                act.wait_ge(he_ready, i * E + e + 1)
                nc.scalar.activation(heh[:, e % 2].rearrange("p c s -> p (c s)"), act_e[:, e % 2, :], ACT.Copy)\
                    .then_inc(he_hi, 1)

            def high(fills, i, t, experts=False):
                name = fills.names[i]
                kind = name[0]
                if kind in ONLY_DVE:
                    return
                bank = ring[fills.bank(i, RING)]
                cd = bank[:].rearrange("p (c d) -> p c d", c=2)
                if kind == "S":
                    act.wait_ge(max_ready, t + 1)
                    for k in range(ST):
                        last = nc.scalar.activation(pr[:, k, :], cd[:, k, :], ACT.Exp, bias=nmax[:, k:k + 1],
                                                    accum_out=rsum[:, k:k + 1])
                    last.then_inc(ring_hi, 1)
                    return
                act.wait_ge(ring_full, fills.at(i) + 1)
                if kind == "H":
                    n = name[1]
                    if n >= 2:
                        act.wait_ge(ring_lo, fills.at(i) + 1 - 2)
                    for k in range(2):
                        last = nc.scalar.activation(gel[n % 2][:, k * S:(k + 1) * S], cd[:, k, :], ACT.Gelu,
                                                    bias=b1_s[:, 2 * n + k:2 * n + k + 1])
                    last.then_inc(gel_ready, 1)
                    act.wait_ge(gel_ready, t * (HC // 2) + n + 1)
                    nc.scalar.activation(hh[:, 2 * n:2 * n + 2, :].rearrange("p c s -> p (c s)"), gel[n % 2],
                                         ACT.Copy).then_inc(ring_hi, 1)
                elif kind in "QK":
                    at, bias = (Q, bq_s) if kind == "Q" else (K, bk_s)
                    for k in range(DC):
                        last = nc.scalar.activation(hh[:, at + k, :], cd[:, k, :], ACT.Identity, bias=bias[:, k:k + 1])
                    last.then_inc(ring_hi, 1)
                elif kind == "R":
                    nc.scalar.activation(sig[:].rearrange("p t e -> p (t e)"), bank[:, 0:ST * E], ACT.Tanh,
                                         scale=thalf[:, 0:1]).then_inc(ring_hi, 1)
                else:
                    if kind == "C" and experts:
                        act.wait_ge(up_full, t * E)
                    dst = {"A": xth[:], "B": xth[:], "C": xch[:], "V": hh[:, V:V + 2, :], "T": hh[:, PT:PT + 2, :]}[kind]
                    nc.scalar.activation(dst, cd, ACT.Copy).then_inc(ring_hi, 1)

            def routing_exps(t):
                act.wait_ge(dist_ready, t + 1)
                nc.scalar.activation(wz[:], dist[:], ACT.Exp, scale=-1.0 / 0.1).then_inc(exps_ready, 1)
                nc.scalar.activation(fb[:], dist[:], ACT.Exp, scale=-1.0 / 0.3).then_inc(exps_ready, 1)

            high(start, 0, 0)
            for k in range(NL):
                weights_high(0, k)
                if k < 3:
                    warm_high(k)
            for n in range(weights.EARLY + 1, E + 1):
                weights.load(act, n)

            def turn(fills, t, experts, nb, nn):
                i = 0

                def highs(names):
                    nonlocal i
                    for _ in names:
                        high(fills, i, t, experts)
                        i += 1

                def steps_of(e, part):
                    for k in PIECES.get((e, part), ()) if nn else ():
                        weights_high(t + 1, k)
                    for k in (LATE if experts else LATE_FIRST).get((e, part), ()) if nb else ():
                        weights_high(t, k)

                for e in range(E):
                    steps_of(e, 0)
                    if e + 1 < E and experts:
                        silu(t - 1, e + 1)
                    elif e + 1 == E and nb:
                        silu(t, 0)
                    before, after = slot(e, nb, nn)
                    if e == 0 and experts:
                        routing_exps(t - 1)
                        hidden_high(t - 1, 1)
                    highs(before[:2])
                    if not experts:
                        for k in warm_pieces(e):
                            warm_high(k)
                    if e == 1 and nb:
                        context_high(t)
                    if 0 < e < E - 1 and experts:
                        hidden_high(t - 1, e + 1)
                    elif e + 1 == E and nb:
                        hidden_high(t, 0)
                    steps_of(e, 1)
                    highs(before[2:])
                    highs(after)
                    steps_of(e, 2)
            sections_of(act, turn)

        @block.vector
        def _(dve):
            def take(s, value):
                dve.wait_ge(s, value)
                dve.sem_inc(took, 1)

            def norm_stats(n, src):
                for k in range(ST):
                    last = nc.vector.bn_stats(stats[:, k, :], src[:, k, :])
                last.then_inc(stats_ready, 1)
                take(stats_ready, n + 1)
                for k in range(ST):
                    last = nc.vector.bn_aggr(mv[:, k, :], stats[:, k, :])
                last.then_inc(var_ready, 1)

            def norm_apply(n, src):
                dve.wait_ge(rstd_ready, n + 1)
                for k in range(ST):
                    last = nc.vector.tensor_scalar(ln[:, k, :], src[:, k, :], mv[:, k, 0:1], rstd[:, k:k + 1],
                                                   ALU.subtract, ALU.mult)
                last.then_inc(ln_ready, 1)

            def weights_sum(n, k):
                dve.wait_ge(stage_in[k % STAGES], piece_in(n, k))
                if k == 0:
                    dve.wait_ge(even_in[0], n * 16 + 16)
                    dve.wait_ge(odd_ready, n + 1)
                for j in range(2):
                    i = k % 2 * 2 + j
                    part = stage[:, k % STAGES, j * D:(j + 1) * D]
                    last = nc.vector.scalar_tensor_tensor(part, even[0][:, i, :], odd[:, k // 2, i:i + 1], part,
                                                          ALU.mult, ALU.add)
                last.then_inc(stage_sum, 1)

            def weights_low(n, k):
                if k < NL:
                    dh, dl = (w[:, k // 2, k % 2 * 2 * D:(k % 2 + 1) * 2 * D] for w in (w1h, w1l))
                else:
                    dh, dl = (w[:, 2 * (k - NL):2 * (k - NL) + 2, :].rearrange("p c d -> p (c d)") for w in (w2h, w2l))
                dve.wait_ge(stage_hi, n * CHUNKS + 2 + k + 1)
                nc.vector.tensor_tensor(dl, stage[:, k % STAGES, :], f32(dh), ALU.subtract).then_inc(stage_lo, 1)

            def warm_low(k):
                dve.wait_ge(warm_hi, k + 1)
                raw, dh, dl = warm_weight(k)
                if k == 0:
                    nc.vector.scalar_tensor_tensor(dl, raw, QSCALE, f32(dh), ALU.mult, ALU.subtract)\
                        .then_inc(warm_lo, 1)
                else:
                    nc.vector.tensor_tensor(dl, raw, f32(dh), ALU.subtract).then_inc(warm_lo, 1)

            def context_low(t):
                dve.wait_ge(ct_hi, t + 1)
                nc.vector.tensor_tensor(ctl[:], ct_raw[:], f32(cth[:]), ALU.subtract).then_inc(ct_lo, 1)

            def hidden(i, e):
                dve.wait_ge(silu_done, i * E + e + 1)
                dve.wait_ge(up_full, i * E + e + 1)
                nc.vector.tensor_tensor(act_e[:, e % 2, :], act_e[:, e % 2, :], ps_u[:], ALU.mult).then_inc(he_ready, 1)

            def hidden_low(i, e):
                dve.wait_ge(he_hi, i * E + e + 1)
                nc.vector.tensor_tensor(hel[:, e % 2].rearrange("p c s -> p (c s)"), act_e[:, e % 2, :],
                                        f32(heh[:, e % 2]).rearrange("p c s -> p (c s)"), ALU.subtract)\
                    .then_inc(he_lo, 1)

            def weigh(i, e):
                dve.wait_ge(down_full, i * E + e + 1)
                if e == 0:
                    dve.wait_ge(wts_ready, i + 1)
                    dve.wait_ge(out_done, i * 16 + 16)
                else:
                    dve.wait_ge(acc_ready, i * E + e + 1)
                for k in range(ST):
                    last = nc.vector.scalar_tensor_tensor(acc[:, k, :], ps_d[:, k * D:(k + 1) * D],
                                                          wts[:, k, e:e + 1], (x2_s if e == 0 else acc)[:, k, :],
                                                          ALU.mult, ALU.add)
                last.then_inc(acc_ready, 1)

            def low(fills, i, t, experts=False):
                name = fills.names[i]
                kind = name[0]
                bank = ring[fills.bank(i, RING)]
                cd = bank[:].rearrange("p (c d) -> p c d", c=2)
                if kind == "Y":
                    dve.wait_ge(ring_full, fills.at(i) + 1)
                    dve.wait_ge(x1_biased, t + 1)
                    if experts:
                        dve.wait_ge(acc_ready, (t - 1) * E + 2)
                    nc.vector.tensor_tensor(x2_s[:], cd, x1_s[:], ALU.add).then_inc(x2_ready, 1)
                    dve.wait_ge(x2_ready, t + 1)
                    dve.sem_inc(ring_lo, 1)
                    return
                if kind == "O":
                    dve.wait_ge(ring_full, fills.at(i) + 1)
                    dve.wait_ge(x2_biased, t + 1)
                    for k in range(ST):
                        last = nc.vector.scalar_tensor_tensor(x2_s[:, k, :], cd[:, k, :], rinv[:, k:k + 1],
                                                              x2_s[:, k, :], ALU.mult, ALU.add)
                    last.then_inc(x3_ready, 1)
                    dve.wait_ge(x3_ready, t + 1)
                    dve.sem_inc(ring_lo, 1)
                    return
                if kind == "S":
                    dve.wait_ge(ring_full, fills.at(i) + 1)
                    nc.vector.tensor_reduce(nmax[:], cd, AX.X, ALU.max, negate=True).then_inc(max_ready, 1)
                    dve.wait_ge(ring_hi, fills.hi_at(i) + 1)
                    nc.vector.reciprocal(rinv[:], rsum[:]).then_inc(ring_lo, 1)
                    return
                dve.wait_ge(ring_hi, fills.hi_at(i) + 1)
                if kind == "H":
                    n = name[1]
                    nc.vector.tensor_tensor(hl[:, 2 * n:2 * n + 2, :].rearrange("p c s -> p (c s)"), gel[n % 2],
                                            f32(hh[:, 2 * n:2 * n + 2, :]).rearrange("p c s -> p (c s)"),
                                            ALU.subtract).then_inc(ring_lo, 1)
                elif kind in "QK":
                    at, bias = (Q, bq_s) if kind == "Q" else (K, bk_s)
                    for k in range(DC):
                        last = nc.vector.scalar_tensor_tensor(hl[:, at + k, :], cd[:, k, :], bias[:, k:k + 1],
                                                              f32(hh[:, at + k, :]), ALU.add, ALU.subtract)
                    last.then_inc(ring_lo, 1)
                elif kind == "R":
                    nc.vector.tensor_scalar(sig[:], sig[:], 0.5, 0.5, ALU.mult, ALU.add).then_inc(ring_lo, 1)
                    dve.wait_ge(ring_lo, fills.at(i) + 1)
                    nc.vector.tensor_scalar(dist[:], sig[:], GOLDEN_CENTER, None, ALU.subtract)
                    nc.vector.tensor_scalar(near[:], sig[:], GOLDEN_LOWER, None, ALU.is_ge).then_inc(route_step, 1)
                    dve.wait_ge(route_step, t * (ROUTE + 1) + 1)
                    nc.vector.scalar_tensor_tensor(near[:], sig[:], GOLDEN_UPPER, near[:], ALU.is_le, ALU.mult)
                    nc.vector.scalar_tensor_tensor(dist[:], dist[:], -1.0, dist[:], ALU.mult, ALU.max)\
                        .then_inc(dist_ready, 1)
                else:
                    dh, dl = {"A": (xth[:], xtl[:]), "B": (xth[:], xtl[:]), "C": (xch[:], xcl[:]),
                              "V": (hh[:, V:V + 2, :], hl[:, V:V + 2, :]),
                              "T": (hh[:, PT:PT + 2, :], hl[:, PT:PT + 2, :])}[kind]
                    if kind == "A":
                        nc.vector.tensor_scalar(odd[:], cd[:, :, 2:2 + 4 * NL:2], lscale[:, 0:1], None, ALU.mult)\
                            .then_inc(odd_ready, 1)
                    nc.vector.tensor_tensor(dl, cd, f32(dh), ALU.subtract).then_inc(ring_lo, 1)

            ROUTE = 14

            def routing(i, part):
                v = nc.vector
                tiles = range(ST)

                def wide(a):
                    return a[:].unsqueeze(2).to_broadcast([P, ST, E])

                stages = [
                    [lambda: v.tensor_tensor(wz[:], wz[:], near[:], ALU.mult)] +
                    [lambda k=k: v.max(top[:, k, :], fb[:, k, :]) for k in tiles],
                    [lambda: v.reduce_sum(wsum[:], wz[:], AX.X)] +
                    [lambda k=k: v.max_index(top_at[:, k, :], top[:, k, :], fb[:, k, :]) for k in tiles],
                    [lambda: v.tensor_scalar(none_in[:], wsum[:], 1e-8, None, ALU.is_lt),
                     lambda: v.tensor_copy(top_f[:], top_at[:, :, 0:2])],
                    [lambda: v.tensor_scalar(some_in[:], none_in[:], -1.0, 1.0, ALU.mult, ALU.add)] +
                    [lambda k=k: v.tensor_scalar(mask[:, k, :], index[:], top_f[:, k, 0:1], None, ALU.is_equal)
                     for k in tiles],
                    [lambda k=k: v.scalar_tensor_tensor(mask[:, k, :], index[:], top_f[:, k, 1:2],
                                                        mask[:, k, :], ALU.is_equal, ALU.add) for k in tiles],
                    [lambda: v.tensor_tensor(fb[:], fb[:], mask[:], ALU.mult),
                     lambda: v.tensor_tensor(wz[:], wz[:], wide(some_in), ALU.mult)],
                    [lambda: v.reduce_sum(fsum[:], fb[:], AX.X)],
                    [lambda: v.tensor_scalar(fsum[:], fsum[:], 1e-8, None, ALU.max)],
                    [lambda: v.reciprocal(fsum[:], fsum[:])],
                    [lambda: v.tensor_tensor(fsum[:], fsum[:], none_in[:], ALU.mult)],
                    [lambda k=k: v.scalar_tensor_tensor(wz[:, k, :], fb[:, k, :], fsum[:, k:k + 1], wz[:, k, :],
                                                        ALU.mult, ALU.add) for k in tiles],
                    [lambda: v.reduce_sum(wsum[:], wz[:], AX.X)],
                    [lambda: v.tensor_scalar(wsum[:], wsum[:], 1e-8, None, ALU.max)],
                    [lambda: v.reciprocal(wsum[:], wsum[:])]]
                assert len(stages) == ROUTE
                if part == 0:
                    take(exps_ready, i * 2 + 2)
                first, last = ((0, 5), (5, 7), (7, 11), (11, ROUTE))[part]
                for n in range(first, last):
                    if n > 0:
                        take(route_step, i * (ROUTE + 1) + 1 + n)
                    for run in stages[n]:
                        ins = run()
                    ins.then_inc(route_step, 1)
                if last == ROUTE:
                    take(route_step, i * (ROUTE + 1) + 1 + ROUTE)
                    v.tensor_tensor(wts[:], wz[:], wide(wsum), ALU.mult).then_inc(wts_ready, 1)

            dve.sem_inc(acc_ready, 1)
            dve.wait_ge(x1_in, 16)
            norm_stats(0, x1_s)
            norm_apply(0, x1_s)
            dve.wait_ge(small_in, 16 * 8)
            nc.vector.reciprocal(tinv[:], tinv[:]).then_inc(w_ready, 1)
            dve.wait_ge(w_ready, 1)
            nc.vector.tensor_scalar(thalf[:], tinv[:], 0.5, None, ALU.mult).then_inc(w_ready, 1)
            dve.wait_ge(stage_hi, 2)
            nc.vector.tensor_tensor(wrl[:], wr_raw[:], f32(wrh[:]), ALU.subtract).then_inc(w_ready, 1)
            low(start, 0, 0)
            for k in range(NL):
                if k < DVE_SUMS:
                    weights_sum(0, k)
                weights_low(0, k)
                if k < 3:
                    warm_low(k)

            def turn(fills, t, experts, nb, nn):
                i = 0

                def lows(names):
                    nonlocal i
                    for _ in names:
                        low(fills, i, t, experts)
                        i += 1

                def steps_of(e, part):
                    for k in PIECES.get((e, part), ()) if nn else ():
                        weights_low(t + 1, k)
                    for k in (LATE if experts else LATE_FIRST).get((e, part), ()) if nb else ():
                        weights_low(t, k)
                    for k in SUMS.get((e, part), ()) if nn else ():
                        weights_sum(t + 1, k)

                for e in range(E):
                    before, after = slot(e, nb, nn)
                    steps_of(e, 0)
                    if e == 5 and nb:
                        if nn:
                            dve.wait_ge(lora_out, t * 16 + 32)
                        norm_apply(ln_no(t, "C"), x2_s)
                    if e + 1 < E and experts:
                        hidden(t - 1, e + 1)
                    elif e + 1 == E and nb:
                        hidden(t, 0)
                    if e == 2 and nb:
                        norm_apply(ln_no(t, "B"), x2_s)
                    if e == 0 and experts:
                        routing(t - 1, 0)
                        hidden_low(t - 1, 1)
                        routing(t - 1, 1)
                        lows(before[:1])
                        routing(t - 1, 2)
                        lows(before[1:2])
                        routing(t - 1, 3)
                    else:
                        lows(before[:2])
                    if not experts:
                        for k in warm_pieces(e):
                            warm_low(k)
                    if e == 1 and nb:
                        context_low(t)
                    if 0 < e < E - 1 and experts:
                        hidden_low(t - 1, e + 1)
                    elif e + 1 == E and nb:
                        hidden_low(t, 0)
                    if e != 5:
                        steps_of(e, 1)
                    if e == 3 and nn:
                        dve.wait_ge(x1_in, t * 16 + 32)
                        norm_stats(ln_no(t, "A"), x1_s)
                    if experts:
                        weigh(t - 1, e)
                    if e == 5:
                        steps_of(e, 1)
                    lows(before[2:])
                    lows(after)
                    if e == 3 and nn:
                        norm_apply(ln_no(t, "A"), x1_s)
                    if e == 1 and nb:
                        norm_stats(ln_no(t, "B"), x2_s)
                    if e == 4 and nb:
                        norm_stats(ln_no(t, "C"), x2_s)
                    steps_of(e, 2)
            sections_of(dve, turn)

        @block.tensor
        def _(pe):
            def product(out, parts, left_h, left_l, right_h, right_l):
                for n, part in enumerate(parts):
                    lh, ll, rh, rl = left_h(part), left_l(part), right_h(part), right_l(part)
                    nc.tensor.matmul(out, lh, rh, start=(n == 0), stop=False)
                    nc.tensor.matmul(out, lh, rl, start=False, stop=False)
                    last = nc.tensor.matmul(out, ll, rh, start=False, stop=(n == len(parts) - 1))
                return last

            def fill(fills, i, t):
                name = fills.names[i]
                kind = name[0]
                bank = ring[fills.bank(i, RING)]
                cd = bank[:].rearrange("p (c d) -> p c d", c=2)
                if fills.turn is not None or fills.first + i >= RING:
                    pe.wait_ge(ring_lo, fills.at(i) + 1 - RING)
                if kind in "ABC":
                    pe.wait_ge(ln_ready, (0 if fills is start else ln_no(t, kind)) + 1)
                    for c in range(DC):
                        for k in range(ST):
                            last = nc.tensor.transpose(cd[:, c, k * P:(k + 1) * P], ln[:, k, c * P:(c + 1) * P], ident[:])
                elif kind == "H":
                    if name[1] == 0:
                        pe.wait_ge(stage_lo, t * CHUNKS + NL)
                        pe.wait_ge(ring_lo, fills.done(("A",), i))
                    for k in range(2):
                        cols = slice((2 * name[1] + k) * P, (2 * name[1] + k + 1) * P)
                        last = product(cd[:, k, :], range(DC), lambda c: w1h[:, c, cols], lambda c: w1l[:, c, cols],
                                       lambda c: xth[:, c, :], lambda c: xtl[:, c, :])
                elif kind == "Y":
                    pe.wait_ge(ring_lo, fills.done(("H", HC // 2 - 1), i))
                    pe.wait_ge(stage_lo, t * CHUNKS + CHUNKS)
                    for k in range(ST):
                        q = slice(k * P, (k + 1) * P)
                        last = product(cd[:, k, :], range(HC), lambda c: hh[:, c, q], lambda c: hl[:, c, q],
                                       lambda c: w2h[:, c, :], lambda c: w2l[:, c, :])
                elif kind in "QK":
                    w, (rh, rl) = (0, (xth, xtl)) if kind == "Q" else (1, (cth, ctl))
                    if kind == "Q":
                        pe.wait_ge(ring_lo, fills.done(("B",), i))
                    else:
                        pe.wait_ge(ct_lo, t + 1)
                        if fills.turn is None and t == 0:
                            pe.wait_ge(warm_lo, 3)
                    for k in range(DC):
                        cols = slice(k * P, (k + 1) * P)
                        last = product(cd[:, k, :], range(DC), lambda c: wqkvh[:, w, c, cols], lambda c: wqkvl[:, w, c, cols],
                                       lambda c: rh[:, c, :], lambda c: rl[:, c, :])
                elif kind == "V":
                    for k in range(ST):
                        q = slice(k * P, (k + 1) * P)
                        last = product(cd[:, k, :], range(DC), lambda c: cth[:, c, q], lambda c: ctl[:, c, q],
                                       lambda c: wqkvh[:, 2, c, :], lambda c: wqkvl[:, 2, c, :])
                elif kind == "S":
                    pe.wait_ge(ring_lo, fills.done(("Q",), i))
                    for k in range(ST):
                        q = slice(k * P, (k + 1) * P)
                        last = product(cd[:, k, :], range(DC), lambda c: hh[:, Q + c, q], lambda c: hl[:, Q + c, q],
                                       lambda c: hh[:, K + c, :], lambda c: hl[:, K + c, :])
                elif kind == "T":
                    pe.wait_ge(ring_lo, fills.done(("S",), i))
                    for k in range(ST):
                        for q in range(ST):
                            last = nc.tensor.transpose(cd[:, k, q * P:(q + 1) * P], pr[:, q, k * P:(k + 1) * P], ident[:])
                elif kind == "O":
                    pe.wait_ge(ring_lo, fills.done(("T",), i))
                    for k in range(ST):
                        q = slice(k * P, (k + 1) * P)
                        last = product(cd[:, k, :], range(ST), lambda c: hh[:, PT + c, q], lambda c: hl[:, PT + c, q],
                                       lambda c: hh[:, V + c, :], lambda c: hl[:, V + c, :])
                else:
                    pe.wait_ge(ring_lo, fills.done(("C",), i))
                    for k in range(ST):
                        q = slice(k * P, (k + 1) * P)
                        last = product(bank[:, k * E:(k + 1) * E], range(DC), lambda c: xch[:, c, q],
                                       lambda c: xcl[:, c, q], lambda c: wrh[:, c, :], lambda c: wrl[:, c, :])
                last.then_inc(ring_full, 1)

            def gate_up(i, e, first=False):
                for w, (ps, full) in enumerate(((ps_g, gate_full), (ps_u, up_full))):
                    if not first:
                        pe.wait_ge(silu_done if w == 0 else he_ready, i * E + e)
                    for k in range(2):
                        cols = slice(k * P, (k + 1) * P)
                        last = product(ps[:, k * S:(k + 1) * S], range(DC), lambda c: weh[:, e, w, c, cols],
                                       lambda c: wel[e][:, w, c, cols], lambda c: xch[:, c, :], lambda c: xcl[:, c, :])
                    last.then_inc(full, 1)

            def down(i, e):
                pe.wait_ge(he_lo, i * E + e + 1)
                pe.wait_ge(acc_ready, i * E + e + 1)
                for k in range(ST):
                    q = slice(k * P, (k + 1) * P)
                    last = product(ps_d[:, k * D:(k + 1) * D], range(2), lambda c: heh[:, e % 2, c, q],
                                   lambda c: hel[:, e % 2, c, q], lambda c: weh[:, e, 2, c, :],
                                   lambda c: wel[e][:, 2, c, :])
                last.then_inc(down_full, 1)

            pe.wait_ge(consts, 2)
            fill(start, 0, 0)
            pe.wait_ge(w_ready, 3)

            def turn(fills, t, experts, nb, nn):
                i = 0
                for e in range(E):
                    if e + 1 < E and experts:
                        gate_up(t - 1, e + 1)
                    elif e + 1 == E and nb:
                        pe.wait_ge(ring_lo, fills.done(("C",), i))
                        if not experts:
                            pe.wait_ge(warm_lo, WARM)
                        gate_up(t, 0, first=not experts)
                    before, after = slot(e, nb, nn)
                    for _ in before:
                        fill(fills, i, t)
                        i += 1
                    if experts:
                        down(t - 1, e)
                    for _ in after:
                        fill(fills, i, t)
                        i += 1
            sections_of(pe, turn)


def program(nc, x, ctx_in, ctxT, a_args, b_args, out, x1, lora):
    with ExitStack() as ctx:
        experts = ExpertWeights(nc, ctx, *b_args)
        latent_attention(nc, x, ctx_in, x1, *a_args, experts.prefetch)
        ffn_attention_experts(nc, x1, ctxT, out, lora, *b_args, experts)


def kernel(x, ctx_1024, L0_xattn_gamma_media, L0_xattn_beta_media, L0_xattn_gamma_lat, L0_xattn_beta_lat, L0_xattn_Wq,
           L0_xattn_bq, L0_xattn_Wkv, L0_xattn_bkv, L0_xattn_Wo, L0_xattn_bo, L0_ffn_W1, L0_ffn_b1, L0_ffn_W2,
           L0_ffn_b2, L0_ffn_scale, L1_xattn_Wq_w, L1_xattn_Wq_b, L1_xattn_Wk_w, L1_xattn_Wk_b, L1_xattn_Wv_w,
           L1_xattn_Wv_b, L1_ffn_Wg, L1_ffn_Wu, L1_ffn_Wd, L1_ffn_Wr, L1_ffn_temperature):
    import numpy as np
    import concourse.bacc as bacc
    from concourse.bass_utils import run_bass_kernel_spmd

    def arr(a):
        return np.asarray(a)

    def cols(a):
        return arr(a).reshape(-1, P).T

    def row(a):
        return arr(a).reshape(1, -1)

    group_a = dict(
        g_media=cols(L0_xattn_gamma_media), b_media=cols(L0_xattn_beta_media), g_lat=cols(L0_xattn_gamma_lat),
        b_lat=cols(L0_xattn_beta_lat), Wq=arr(L0_xattn_Wq), bq=cols(L0_xattn_bq), Wkv=arr(L0_xattn_Wkv),
        bkv=arr(L0_xattn_bkv).reshape(2, -1, P).transpose(2, 0, 1), Wo=arr(L0_xattn_Wo), bo=row(L0_xattn_bo))
    group_b = dict(
        W1T=arr(L0_ffn_W1).T, b1=cols(L0_ffn_b1), W2T=arr(L0_ffn_W2).T, b2=row(L0_ffn_b2), scale=row(L0_ffn_scale),
        WqT=arr(L1_xattn_Wq_w).T, bq1=cols(L1_xattn_Wq_b), WkT=arr(L1_xattn_Wk_w).T, bk1=cols(L1_xattn_Wk_b),
        WvT=arr(L1_xattn_Wv_w).T, bv1=row(L1_xattn_Wv_b), Wg=arr(L1_ffn_Wg), Wu=arr(L1_ffn_Wu), Wd=arr(L1_ffn_Wd),
        Wr=arr(L1_ffn_Wr), temp=row(L1_ffn_temperature))
    tokens = dict(x=arr(x), ctx_in=arr(ctx_1024), ctxT=arr(ctx_1024).transpose(0, 2, 1))

    nc = bacc.Bacc("TRN2", target_bir_lowering=False, num_devices=1)
    arrays, aps = {}, {}
    for name, a in {**tokens, **group_a, **group_b}.items():
        a = np.ascontiguousarray(a)
        arrays["in_" + name] = a
        aps[name] = nc.dram_tensor("in_" + name, a.shape, mybir.dt.from_np(a.dtype), kind="ExternalInput").ap()
    out = nc.dram_tensor("out_x", (B, S, D), F32, kind="ExternalOutput").ap()
    x1 = nc.dram_tensor("x1_between", (B, S, D), F32, kind="Internal").ap()
    lora = nc.dram_tensor("lora_rows", (B, 16, D), F32, kind="Internal").ap()
    program(nc, aps["x"], aps["ctx_in"], aps["ctxT"], [aps[n] for n in group_a], [aps[n] for n in group_b], out, x1,
            lora)
    r = run_bass_kernel_spmd(nc, [arrays], core_ids=[0])
    return r.results[0]["out_x"]
```
